# Optimizing a Trainium2 kernel written in Bass

```python
import numpy as np
import jax
import jax.numpy as jnp

def _softmax(x, axis=-1):
    return jax.nn.softmax(x, axis=axis)

def _gelu(x):
    return jax.nn.gelu(x, approximate=True)

def _silu(x):
    return jax.nn.silu(x)

def _sigmoid(x):
    return jax.nn.sigmoid(x)

def _layernorm(x, axis=-1, eps=1e-05):
    m = jnp.mean(x, axis=axis, keepdims=True)
    v = jnp.var(x, axis=axis, keepdims=True)
    return (x - m) / jnp.sqrt(v + eps)

def _scatter_add(tgt, idx, src, axis=0):
    return tgt.at[idx].add(src)

def _segment_sum(src, seg, n):
    return jax.ops.segment_sum(src, seg, n)
kernel_name = 'mk_adj_resnorm_d4_adj_r2_aa7710'

def setup_inputs(seed: int=0):
    np.random.seed(seed)
    _w = jnp.asarray

    def _rec_inputs():
        import jax
        import jax.numpy as jnp
        _gk = jax.random.key(seed)
        x = -0.0005207 + 1.001 * jax.random.normal(jax.random.fold_in(_gk, 1), (64, 128, 128), jnp.float32)
        _a = jax.random.bernoulli(jax.random.fold_in(_gk, 2), 0.125, (64, 128, 128))
        _af = _a.astype(jnp.float32)
        adj = _af
        return (x, adj)
    x, adj = _rec_inputs()

    def _L0_gnn_setup():
        import jax, jax.numpy as jnp
        import numpy as np
        BS, N, F = (8, 1024, 128)
        key = jax.random.key(seed)
        k1, k2, k3, k4 = jax.random.split(key, 4)
        node_embedding = jax.random.normal(k1, (BS, N, F), dtype=jnp.float32)
        att_mat = jax.random.randint(k2, (BS, N, N), 0, 2).astype(jnp.float32)
        W = jax.random.normal(k3, (F, F), dtype=jnp.float32) * 0.05
        a = jax.random.normal(k4, (2 * F,), dtype=jnp.float32) * 0.05
        return {'node_embedding': node_embedding, 'att_mat': att_mat, 'W': W, 'a': a}
    _L0_gnn_all = _L0_gnn_setup()
    _L0_gnn_in = {k: v for k, v in _L0_gnn_all.items() if k in ('W', 'a')}
    del _L0_gnn_all

    def _L1_gnn_setup():
        import jax, jax.numpy as jnp
        import numpy as np
        NEG_SLOPE = 0.2
        key = jax.random.key(seed)
        k1, k2, k3, k4 = jax.random.split(key, 4)
        B, n, d_in, d_out = (8, 1024, 128, 128)
        x = jax.random.normal(k1, (B, n, d_in), dtype=jnp.float32)
        adj = jax.random.uniform(k2, (B, n, n), dtype=jnp.float32)
        W = jax.random.normal(k3, (d_in, d_out), dtype=jnp.float32) * np.sqrt(2.0 / (d_in + d_out))
        a = jax.random.normal(k4, (2 * d_out,), dtype=jnp.float32) * np.sqrt(2.0 / (2 * d_out + 1))
        return {'x': x, 'adj': adj, 'W': W, 'a': a}
    _L1_gnn_all = _L1_gnn_setup()
    _L1_gnn_in = {k: v for k, v in _L1_gnn_all.items() if k in ('W', 'a')}
    del _L1_gnn_all

    def _L2_gnn_setup():
        import jax, jax.numpy as jnp
        import numpy as np
        B, N, IN_F = (4, 256, 128)
        H, F = (8, 16)
        SLOPE = 0.2
        key = jax.random.key(seed)
        k1, k2, k3, k4, k5 = jax.random.split(key, 5)
        h = jax.random.normal(k1, (B, N, IN_F), dtype=jnp.float32)
        adj = jax.random.randint(k2, (B, N, N), 0, 2).astype(jnp.float32)
        eye = jnp.eye(N, dtype=jnp.float32)[None]
        adj = jnp.maximum(adj, eye)
        W_l = jax.random.normal(k3, (H * F, IN_F), dtype=jnp.float32) * 0.05
        W_r = jax.random.normal(k4, (H * F, IN_F), dtype=jnp.float32) * 0.05
        w_attn = jax.random.normal(k5, (F,), dtype=jnp.float32) * 0.05
        return {'h': h, 'adj_mat': adj, 'W_l': W_l, 'W_r': W_r, 'w_attn': w_attn}
    _L2_gnn_all = _L2_gnn_setup()
    _L2_gnn_in = {k: v for k, v in _L2_gnn_all.items() if k in ('W_l', 'W_r', 'w_attn')}
    del _L2_gnn_all

    def _L3_gnn_setup():
        import jax, jax.numpy as jnp
        import numpy as np
        import math
        CUTOFF = 5.0
        LOG2 = math.log(2.0)

        def ssp(x):
            return jax.nn.softplus(x) - LOG2
        key = jax.random.key(seed)
        ks = jax.random.split(key, 12)
        B, A, C, F, R = (4, 256, 128, 128, 20)
        x = jax.random.normal(ks[0], (B, A, C), dtype=jnp.float32)
        d_ij = jax.random.uniform(ks[1], (B, A, A), dtype=jnp.float32) * 6.0
        widths = jnp.linspace(1.0, CUTOFF, R, dtype=jnp.float32)
        offsets = jnp.zeros((R,), dtype=jnp.float32)
        s = lambda k, shp: jax.random.normal(k, shp, dtype=jnp.float32) * 0.05
        w_in2f = s(ks[2], (C, F))
        fw1, fb1 = (s(ks[3], (R, F)), jnp.zeros((F,), jnp.float32))
        fw2, fb2 = (s(ks[4], (F, F)), jnp.zeros((F,), jnp.float32))
        ow1, ob1 = (s(ks[5], (F, C)), jnp.zeros((C,), jnp.float32))
        ow2, ob2 = (s(ks[6], (C, C)), jnp.zeros((C,), jnp.float32))
        return dict(x=x, d_ij=d_ij, widths=widths, offsets=offsets, w_in2f=w_in2f, fw1=fw1, fb1=fb1, fw2=fw2, fb2=fb2, ow1=ow1, ob1=ob1, ow2=ow2, ob2=ob2)
    _L3_gnn_all = _L3_gnn_setup()
    _L3_gnn_in = {k: v for k, v in _L3_gnn_all.items() if k in ('widths', 'offsets', 'w_in2f', 'fw1', 'fb1', 'fw2', 'fb2', 'ow1', 'ob1', 'ow2', 'ob2')}
    del _L3_gnn_all
    return {'x': x, 'adj': adj, 'L0_gnn_W': _L0_gnn_in['W'], 'L0_gnn_a': _L0_gnn_in['a'], 'L1_gnn_W': _L1_gnn_in['W'], 'L1_gnn_a': _L1_gnn_in['a'], 'L2_gnn_W_l': _L2_gnn_in['W_l'], 'L2_gnn_W_r': _L2_gnn_in['W_r'], 'L2_gnn_w_attn': _L2_gnn_in['w_attn'], 'L3_gnn_widths': _L3_gnn_in['widths'], 'L3_gnn_offsets': _L3_gnn_in['offsets'], 'L3_gnn_w_in2f': _L3_gnn_in['w_in2f'], 'L3_gnn_fw1': _L3_gnn_in['fw1'], 'L3_gnn_fb1': _L3_gnn_in['fb1'], 'L3_gnn_fw2': _L3_gnn_in['fw2'], 'L3_gnn_fb2': _L3_gnn_in['fb2'], 'L3_gnn_ow1': _L3_gnn_in['ow1'], 'L3_gnn_ob1': _L3_gnn_in['ob1'], 'L3_gnn_ow2': _L3_gnn_in['ow2'], 'L3_gnn_ob2': _L3_gnn_in['ob2']}

def reference(x, adj, L0_gnn_W, L0_gnn_a, L1_gnn_W, L1_gnn_a, L2_gnn_W_l, L2_gnn_W_r, L2_gnn_w_attn, L3_gnn_widths, L3_gnn_offsets, L3_gnn_w_in2f, L3_gnn_fw1, L3_gnn_fb1, L3_gnn_fw2, L3_gnn_fb2, L3_gnn_ow1, L3_gnn_ob1, L3_gnn_ow2, L3_gnn_ob2):
    import jax
    import jax.numpy as jnp

    def _L0_gnn_ref(node_embedding, att_mat, W, a):
        import jax, jax.numpy as jnp
        import numpy as np
        BS, N, F = (8, 1024, 128)
        h = jnp.einsum('bnf,fo->bno', node_embedding, W)
        f = a.shape[0] // 2
        s1 = h @ a[:f]
        s2 = h @ a[f:]
        alpha = jnp.tanh(s1[:, :, None] + s2[:, None, :])
        NEG_INF = jnp.float32(-1000000000000000.0)
        attn = jnp.where(att_mat > 0, alpha, NEG_INF)
        attn = jax.nn.softmax(attn, axis=-1)
        last_h = jnp.einsum('bij,bjf->bif', attn, h)
        su = jnp.sum(att_mat, axis=1)[:, :, None]
        return jnp.where(su == 0, node_embedding, last_h)

    def _L1_gnn_ref(x, adj, W, a):
        import jax, jax.numpy as jnp
        import numpy as np
        NEG_SLOPE = 0.2
        d_out = W.shape[1]
        h = jnp.einsum('bni,io->bno', x, W)
        x_weighted = jnp.einsum('bnm,bmo->bno', adj, h)
        a_src, a_dst = (a[:d_out], a[d_out:])
        s_i = h @ a_src
        s_j = h @ a_dst
        e = jax.nn.leaky_relu(s_i[:, :, None] + s_j[:, None, :], NEG_SLOPE)
        alpha = jax.nn.softmax(e, axis=2)
        out = jnp.einsum('bnm,bmo->bno', alpha, h) + x_weighted
        return jax.nn.leaky_relu(out, NEG_SLOPE)

    def _L2_gnn_ref(h, adj_mat, W_l, W_r, w_attn):
        import jax, jax.numpy as jnp
        import numpy as np
        B, N, IN_F = (4, 256, 128)
        H, F = (8, 16)
        SLOPE = 0.2
        b, n, _ = h.shape
        g_l = (h @ W_l.T).reshape(b, n, H, F)
        g_r = (h @ W_r.T).reshape(b, n, H, F)
        g_sum = g_r[:, :, None, :, :] + g_l[:, None, :, :, :]
        e = jnp.einsum('bijhf,f->bijh', jax.nn.leaky_relu(g_sum, SLOPE), w_attn)
        mask = adj_mat[..., None]
        e = e * mask
        e = jnp.where(mask == 0, -jnp.inf, e)
        a = jax.nn.softmax(e, axis=2)
        attn_res = jnp.einsum('bijh,bjhf->bihf', a, g_r)
        out = jax.nn.leaky_relu(attn_res.reshape(b, n, H * F), SLOPE)
        return out

    def _L3_gnn_ref(x, d_ij, widths, offsets, w_in2f, fw1, fb1, fw2, fb2, ow1, ob1, ow2, ob2):
        import jax, jax.numpy as jnp
        import numpy as np
        import math
        CUTOFF = 5.0
        LOG2 = math.log(2.0)

        def ssp(x):
            return jax.nn.softplus(x) - LOG2
        coeff = -0.5 / (widths * widths)
        diff = d_ij[..., None] - offsets
        f_ij = jnp.exp(coeff * diff * diff)
        rcut = 0.5 * (jnp.cos(d_ij * (math.pi / CUTOFF)) + 1.0) * (d_ij < CUTOFF).astype(d_ij.dtype)
        y = x @ w_in2f
        W = ssp(f_ij @ fw1 + fb1) @ fw2 + fb2
        W = W * rcut[..., None]
        agg = jnp.einsum('bjf,bijf->bif', y, W)
        out = ssp(agg @ ow1 + ob1) @ ow2 + ob2
        return out
    x = _layernorm(x + _L0_gnn_ref(x, adj, L0_gnn_W, L0_gnn_a), axis=-1)
    x = _layernorm(x + _L1_gnn_ref(x, adj, L1_gnn_W, L1_gnn_a), axis=-1)
    x = _layernorm(x + _L2_gnn_ref(x, adj, L2_gnn_W_l, L2_gnn_W_r, L2_gnn_w_attn), axis=-1)
    x = _layernorm(x + _L3_gnn_ref(x, adj, L3_gnn_widths, L3_gnn_offsets, L3_gnn_w_in2f, L3_gnn_fw1, L3_gnn_fb1, L3_gnn_fw2, L3_gnn_fb2, L3_gnn_ow1, L3_gnn_ob1, L3_gnn_ow2, L3_gnn_ob2), axis=-1)
    return x

_drawn_inputs = setup_inputs


def setup_inputs(seed=0):
    import zlib

    import numpy as np

    out = dict(_drawn_inputs(seed))
    spreads = {'L3_gnn_offsets': (0.0, 0.8),
     'L3_gnn_fb1': (0.0, 0.1),
     'L3_gnn_fb2': (0.0, 0.1),
     'L3_gnn_ob1': (0.0, 0.303),
     'L3_gnn_ob2': (0.0, 0.1)}
    factors = {'L2_gnn_W_l': 6.29, 'L2_gnn_w_attn': 5.302, 'L3_gnn_widths': 8.0}
    for name, (base, spread) in spreads.items():
        noise = np.random.default_rng([zlib.crc32(name.encode()), seed]).standard_normal(out[name].shape)
        drawn = base * np.exp(spread * noise) if base else spread * noise
        out[name] = jnp.asarray(drawn.astype(out[name].dtype))
    for name, factor in factors.items():
        out[name] = (out[name] * factor).astype(out[name].dtype)
    return out
```

```python
import math
from contextlib import ExitStack

import concourse.bass as bass
from concourse import mybir

FP32 = mybir.dt.float32
BF16 = mybir.dt.bfloat16
I32 = mybir.dt.int32
ALU = mybir.AluOpType
ACT = mybir.ActivationFunctionType
X = mybir.AxisListType.X

B = 64
N = 128
F = 128
H = 8
FH = F // H
R = 20
SLOPE = 0.2
EPS = 1e-5
LOG2 = math.log(2.0)
CUTOFF = 5.0
CUT0 = 1.0
CUT1 = 0.5 * (math.cos(math.pi / CUTOFF) + 1.0)
QUAD = 4
QUADS = B // QUAD
MASKED = 1.0e30
ROUNDER = 1.5 * 2.0 ** 23
RING = 4
STEPS = 8
LAST_STAGE = 4
HE = FH + 1

TILES = 16
DVE_TILES = [9] * STEPS
ACT_TILES = [2, 1, 2, 1, 2, 1, 2, 1]


class Item:

    def __init__(self, turn, offset, body=RING, total=B):
        self.turn, self.offset, self.body, self.total = turn, offset, body, total
        self.static = isinstance(turn, int)
        self.slot4, self.slot2 = offset % 4, offset % 2

    def there(self):
        return not self.static or 0 <= self.body * self.turn + self.offset < self.total

    def count(self, per_item=1, plus=0):
        return (self.body * per_item) * self.turn + (per_item * self.offset + plus)

    def loads(self, slots=RING):
        return (16 * self.body // slots) * self.turn + 16 * (self.offset // slots + 1)

    def columns(self, width=F):
        start = (self.body * width) * self.turn + width * self.offset
        return slice(start, start + width) if self.static else bass.ds(start, width)

    def pick(self, array):
        if self.static:
            return array[self.body * self.turn + self.offset]
        return array[bass.ds(self.body * self.turn + self.offset, 1)].rearrange("a n f -> (a n) f")


class Chain:

    def __init__(self, semaphore, names, turns):
        self.semaphore, self.names, self.turns = semaphore, names.split(), turns

    def after(self, name, outer, turn=0):
        stages = len(self.names)
        index = 0 if name == "start" else self.names.index(name) + 1
        return (stages * self.turns + 1) * outer + stages * turn + (index + 1)


GRAPH_STAGES = """
    turned0 turned0_kept projected0 h0 scores0 edges0 masked0 max0 probs0 probsT0 probsT0_kept attended0 recip0 weight0
    norm0 added0 moments0 seen0 var0 vareps0 rstd0 layer0
    turned1 turned1_kept projected1 h1 scores1 lrelu1 max1 probs1 probsT1 probsT1_kept attended1 recip1 norm1 mixed1
    act1 added1 moments1 seen1 var1 vareps1 rstd1 layer1
    turned2 turned2_kept projected2 projected2_kept pairs
    turned_scores2 weighed2 masked2 max2 shifted2 exps2 edges2 sums2 probsT2 probsT2_kept attended2 recips2 norm2 act2
    added2 moments2 seen2 var2 vareps2 rstd2 layer2
    turned3 turned3_kept projected3 projected3_kept rows hidden3 bias3 abs3 exp3 ln3 softplus3 output3
    added3 moments3 seen3 var3 vareps3 rstd3 layer3
    stored"""
PAIR_STAGES = "added lrelu summed kept"
ROW_STAGES = """
    offset squares exponents rest radial hidden bias abs exp ln softplus ssp filter
    size cosine raised cut weighed messages kept"""


def wait(engine, semaphore, value, most=None):
    if isinstance(value, int):
        if value <= 0:
            return
        if most is not None:
            value = min(value, most)
    engine.wait_ge(semaphore, value)


def build(nc, x, adj, W0, a0, W1, a1, W_l, W_r, w_attn, widths, offsets, w_in2f, fw1, fb1, fw2, fb2,
          ow1, ob1, ow2, ob2, ident_in, heads_in, out):
    ctx = ExitStack()
    with ctx:
        def sb(name, shape, dt=FP32):
            return ctx.enter_context(nc.sbuf_tensor(name, shape, dt))

        def sem(name):
            return ctx.enter_context(nc.semaphore(name))

        ident = sb("ident", [N, N])
        heads = sb("heads", [F, H])
        raw = sb("raw", [F, 8, F])
        vec = sb("vec", [F, 16])
        w0x = sb("w0x", [F, F + 1])
        w1x = sb("w1x", [F, F + 1])
        src0 = sb("src0", [F, N])
        src1 = sb("src1", [F, N])
        dst1 = sb("dst1", [F, N])
        wcol = sb("wcol", [F, 4])
        wlT = sb("wlT", [F, F])
        wrT = sb("wrT", [F, F])
        wrnT = sb("wrnT", [F, F])
        sgn = sb("sgn", [F, 4])
        sgn8 = sb("sgn8", [F, H])
        ssum = sb("ssum", [F, 4, 32])
        slin = sb("slin", [F, 16, H])
        rows = sb("rows", [N, H, 16, H], BF16)
        win = sb("win", [F, F])
        w1f = sb("w1f", [R, F])
        w2f = sb("w2f", [F, F])
        ow1s = sb("ow1s", [F, F])
        ow2s = sb("ow2s", [F, F])
        radial = sb("radial", [R, 8])
        ones = sb("ones", [N, N])
        filt = sb("filt", [F, 12])
        halves = sb("halves", [N, QUAD])
        epses = sb("epses", [N, QUAD])
        brow = sb("brow", [1, 5, F])

        xin = sb("xin", [N, RING, F])
        adj_a = sb("adj_a", [N, RING, N])
        adj_b = sb("adj_b", [N, RING, N])
        xa = sb("xa", [N, 2, 2 * N])
        h0 = sb("h0", [N, 2, F + 2])
        tanh0 = sb("tanh0", [N, 2, N])
        exp0 = sb("exp0", [N, 2, N])
        prob0 = sb("prob0", [N, 2, N])
        chk = sb("chk", [N, 2, N])
        small = sb("small", [N, 2, 64])
        sum0 = sb("sum0", [N, 2, F])
        x1 = sb("x1", [N, 2, F])
        x1T = sb("x1T", [F, 2, N])
        h1 = sb("h1", [N, 2, F + 2])
        relu1 = sb("relu1", [N, 2, N])
        max1 = sb("max1", [N, 2, N])
        dif1 = sb("dif1", [N, 2, N])
        prob1 = sb("prob1", [N, 2, N])
        nbr1 = sb("nbr1", [N, 2, F])
        mix1 = sb("mix1", [N, 2, F])
        act1 = sb("act1", [N, 2, F])
        sum1 = sb("sum1", [N, 2, F])
        x2 = sb("x2", [N, RING, F])
        x2T = sb("x2T", [F, 2, N])
        gl = sb("gl", [F, 2, N])
        gr = sb("gr", [F, 2, N])
        ngr = sb("ngr", [F, 2, N])
        grx = sb("grx", [N, 2, H, HE])
        Z = sb("Z", [F, 2, 4, TILES, N])
        maskb = sb("maskb", [N, 2, N], BF16)
        negmax = sb("negmax", [N, 2, 8])
        prob2 = sb("prob2", [N, 2, 4, N])
        pT = sb("pT", [N, 4, 4, 2, 32])
        att2 = sb("att2", [N, 2, H, FH])
        act2 = sb("act2", [N, 2, F])
        sum2 = sb("sum2", [N, 2, F])
        x3 = sb("x3", [N, 2, F])
        xa3 = sb("xa3", [N, 2, 2 * N + 1])
        y3 = sb("y3", [N, 2, F])
        ysum = sb("ysum", [F, 2, 1])
        x3_all = sb("x3_all", [N, B * F])
        agg_all = sb("agg_all", [F, B * N])
        chk_all = sb("chk_all", [N, B])
        sum_all = sb("sum_all", [N, B])
        deg_all = sb("deg_all", [N, B])
        verdict = sb("verdict", [N, 8])
        flag = sb("flag", [1, 1], I32)

        bank = [ctx.enter_context(nc.psum_tensor(f"bank{i}", [128, 512], FP32)) for i in range(8)]
        X0, X1, X2, T = bank[0], bank[1], bank[2], bank[3]
        GL = bank[4:6]
        E = bank[6:8]

        s_w = sem("weights_loaded")
        s_ones = sem("ones_set")
        s_own = sem("vector_own_order")
        s_wT = sem("w0_w1_transposed")
        s_wTC = sem("w0_w1_transposed_copied")
        s_wa = sem("w_times_a")
        s_scl = sem("w_l_w_r_scaled")
        s_wlr = sem("w_l_w_r_transposed")
        s_rade = sem("radial_exponents")
        s_rad = sem("radial_values")
        s_hid = sem("filter_hidden")
        s_hidb = sem("filter_hidden_bias")
        s_soft = sem("filter_softplus")
        s_ssp = sem("filter_ssp")
        s_fil = sem("filter_values")
        s_ready = sem("constants_ready")
        s_x = [sem(f"x_loaded{i}") for i in range(RING)]
        s_aa = [sem(f"adj_a_loaded{i}") for i in range(RING)]
        s_ab = [sem(f"adj_b_loaded{i}") for i in range(RING)]
        s_xaT = sem("x_adj_transposed")
        s_xaC = sem("x_adj_copied")
        s_p0 = sem("projected0")
        s_h0 = sem("h0_copied")
        s_th = sem("tanh_done")
        s_e0 = sem("exp0_done")
        s_pr0 = sem("prob0_done")
        s_at0 = sem("attended0")
        s_rs0 = sem("recip0")
        s_sm0 = sem("sum0_done")
        s_st0 = sem("stats0")
        s_ag0 = sem("var0")
        s_ve0 = sem("var0_eps")
        s_rd0 = sem("rstd0")
        s_x1 = sem("x1_done")
        s_ck = sem("chk_product")
        s_ck2 = sem("chk_done")
        s_lc = sem("sum_kept")
        s_x1T = sem("x1_transposed")
        s_x1C = sem("x1T_copied")
        s_p1 = sem("projected1")
        s_mx1 = sem("smax_done")
        s_h1 = sem("h1_copied")
        s_u1 = sem("relu1_done")
        s_m1 = sem("max1_done")
        s_d1 = sem("dif1_done")
        s_e1 = sem("prob1_done")
        s_at1 = sem("attended1")
        s_nb1 = sem("nbr1_copied")
        s_rs1 = sem("recip1")
        s_mix1 = sem("mix1_done")
        s_act1 = sem("act1_done")
        s_sm1 = sem("sum1_done")
        s_st1 = sem("stats1")
        s_ag1 = sem("var1")
        s_ve1 = sem("var1_eps")
        s_rd1 = sem("rstd1")
        s_x2 = sem("x2_done")
        s_x2T = sem("x2_transposed")
        s_x2C = sem("x2T_copied")
        s_p2 = sem("projected2")
        s_gl = sem("gl_copied")
        s_gr = sem("gr_copied")
        s_ngr = sem("ngr_copied")
        s_grx = sem("grx_copied")
        s_mb = sem("mask_bias")
        s_zv = sem("tiles_vector")
        s_za = sem("tiles_scalar")
        s_zp = sem("tiles_pool")
        s_zu = sem("tiles_summed")
        s_sc = sem("scores_done")
        s_mx2 = sem("max2_done")
        s_e2 = sem("prob2_done")
        s_pT = sem("prob2_transposed")
        s_pC = sem("pT_copied")
        s_at2 = sem("attended2")
        s_rs2 = sem("recip2")
        s_nm2 = sem("att2_done")
        s_act2 = sem("act2_done")
        s_sm2 = sem("sum2_done")
        s_st2 = sem("stats2")
        s_ag2 = sem("var2")
        s_ve2 = sem("var2_eps")
        s_rd2 = sem("rstd2")
        s_x3 = sem("x3_done")
        s_x3k = [sem(f"x3_kept{i}") for i in range(2)]
        s_x3T = sem("x3_adj_transposed")
        s_x3C = sem("x3_adj_copied")
        s_y3 = sem("y3_projected")
        s_y3C = sem("y3_copied")
        s_ag3 = sem("aggregated3")
        s_ys = sem("ysum_done")
        s_agC = sem("agg_kept")

        s_cst = sem("minus_half_set")
        s_bz = sem("out_hidden")
        s_bzb = sem("out_hidden_bias")
        s_ba = sem("out_abs")
        s_be = sem("out_exp")
        s_bl = sem("out_log")
        s_bmx = sem("out_ssp")
        s_bo = sem("out_projected")
        s_br = sem("out_residual")
        s_bs = sem("out_stats")
        s_bv = sem("out_var")
        s_bve = sem("out_var_eps")
        s_brd = sem("out_rstd")
        s_bnb = sem("out_shift")
        s_by = sem("out_normed")
        s_store = [sem(f"stored{i}") for i in range(2)]

        space = Z[:, :, :, :, :].rearrange("p a b c j -> p (a b c j)")

        def last(k):
            return space[:, k * 2 * QUAD * N:(k + 1) * 2 * QUAD * N].rearrange("p (a n) -> p a n", a=2)

        zb, absz, expz, lnz, ssp, res, fin = (last(k) for k in range(7))
        mom = sb("mom", [N, 2, QUAD, 16])

        block = ctx.enter_context(nc.Block())

        def bcast(ap, shape):
            return ap.to_broadcast(shape)


        def in_last_phase(engine, period):
            for u in range(2):
                period(0, u)
            with engine.Fori(1, QUADS // 2) as pair:
                for u in range(2):
                    period(pair, u)
            period(QUADS // 2, 0)

        def last_phase_sync(sp):
            def period(pair, u):
                b = Item(pair, u - 1, 2, QUADS)
                if b.there():
                    wait(sp, s_by, b.count(plus=1))
                    source = fin[:, b.slot2, :].rearrange("p (g f) -> p g f", g=QUAD)
                    if b.static:
                        first = QUAD * (2 * b.turn + b.offset)
                        to = out[first:first + QUAD]
                    else:
                        to = out[bass.ds(QUAD * 2 * b.turn + QUAD * b.offset, QUAD)]
                    sp.dma_start(to.rearrange("g n f -> n g f"), source).then_inc(s_store[b.slot2], 16)

            in_last_phase(sp, period)
            for k in range(2):
                sp.wait_ge(s_store[k], 16 * QUADS // 2)

        def last_phase_tensor(pe):
            mm = nc.tensor.matmul
            pe.wait_ge(s_agC, B)
            banks = [X0, X1]
            outs = [X2, T]

            def period(pair, u):
                a, b = Item(pair, u, 2, QUADS), Item(pair, u - 1, 2, QUADS)
                if a.there():
                    wait(pe, s_bzb, a.count(plus=-1))
                    mm(banks[a.slot2][:, :], ow1s[:, :], agg_all[:, a.columns(QUAD * N)], start=True, stop=True)\
                        .then_inc(s_bz, 1)
                if b.there():
                    wait(pe, s_bmx, b.count(plus=1))
                    wait(pe, s_br, b.count(plus=-1))
                    mm(outs[b.slot2][:, :], ones[0:1, :], brow[0:1, 0:QUAD, :].rearrange("p k f -> p (k f)"),
                       start=True, stop=False, skip_group_check=True)
                    for g in range(QUAD):
                        ins = mm(outs[b.slot2][:, g * F:(g + 1) * F], ssp[:, b.slot2, g * N:(g + 1) * N], ow2s[:, :],
                                 start=False, stop=True, skip_group_check=True)
                    ins.then_inc(s_bo, 1)

            in_last_phase(pe, period)

        def last_phase_scalar(act):
            A = nc.scalar.activation

            def period(pair, u):
                a, b = Item(pair, u, 2, QUADS), Item(pair, u - 1, 2, QUADS)
                if a.there():
                    wait(act, s_bzb, a.count(plus=1))
                    A(absz[:, a.slot2, :], zb[:, a.slot2, :], ACT.Abs).then_inc(s_ba, 1)
                if a.there():
                    wait(act, s_ba, a.count(plus=1))
                    A(expz[:, a.slot2, :], absz[:, a.slot2, :], ACT.Exp, scale=-1.0).then_inc(s_be, 1)
                if a.there():
                    wait(act, s_be, a.count(plus=1))
                    wait(act, s_bmx, a.count(plus=-1))
                    A(lnz[:, a.slot2, :], expz[:, a.slot2, :], ACT.Ln, bias=1.0).then_inc(s_bl, 1)
                if b.there():
                    wait(act, s_bnb, b.count(plus=1))
                    wait(act, s_store[b.slot2], b.loads(2) - 16)
                    for g in range(QUAD):
                        ins = A(fin[:, b.slot2, g * F:(g + 1) * F], res[:, b.slot2, g * F:(g + 1) * F], ACT.Identity,
                                scale=mom[:, b.slot2, g, 9:10], bias=mom[:, b.slot2, g, 10:11])
                    ins.then_inc(s_by, 1)

            in_last_phase(act, period)

        def last_phase_vector(dve):
            V = nc.vector
            dve.wait_ge(s_x3k[0], 16 * B // 2)
            dve.wait_ge(s_x3k[1], 16 * B // 2)

            def period(pair, u):
                a, b = Item(pair, u, 2, QUADS), Item(pair, u - 1, 2, QUADS)
                if a.there():
                    wait(dve, s_bz, a.count(plus=1))
                    wait(dve, s_ba, a.count(plus=-1))
                    wait(dve, s_zu, B * STEPS)
                    V.tensor_scalar(zb[:, a.slot2, :], (X0, X1)[a.slot2][:, :], vec[:, 6:7], None, ALU.add)\
                        .then_inc(s_bzb, 1)
                if b.there():
                    wait(dve, s_bo, b.count(plus=1))
                    wait(dve, s_by, b.count(plus=-1))
                    V.tensor_tensor(res[:, b.slot2, :], (X2, T)[b.slot2][:, :], x3_all[:, b.columns(QUAD * F)],
                                    ALU.add).then_inc(s_br, 1)
                    wait(dve, s_br, b.count(plus=1))
                    for g in range(QUAD):
                        ins = V.bn_stats(mom[:, b.slot2, g, 0:6], res[:, b.slot2, g * F:(g + 1) * F])
                    ins.then_inc(s_bs, 1)
                    wait(dve, s_bs, b.count(plus=1))
                if a.there():
                    wait(dve, s_bl, a.count(plus=1))
                    wait(dve, s_bo, a.count(plus=-1))
                    V.scalar_tensor_tensor(ssp[:, a.slot2, :], zb[:, a.slot2, :], 0.0, lnz[:, a.slot2, :], ALU.max,
                                           ALU.add).then_inc(s_bmx, 1)
                if b.there():
                    for g in range(QUAD):
                        ins = V.bn_aggr(mom[:, b.slot2, g, 6:8], mom[:, b.slot2, g, 0:6])
                    ins.then_inc(s_bv, 1)
                    wait(dve, s_brd, b.count(plus=1))
                    V.scalar_tensor_tensor(mom[:, b.slot2, :, 10], mom[:, b.slot2, :, 6], -1.0,
                                           mom[:, b.slot2, :, 9], ALU.mult, ALU.mult).then_inc(s_bnb, 1)

            in_last_phase(dve, period)

        def last_phase_pool(pool):
            G = nc.gpsimd

            def period(pair, u):
                b = Item(pair, u - 1, 2, QUADS)
                if b.there():
                    wait(pool, s_bv, b.count(plus=1))
                    G.tensor_tensor(mom[:, b.slot2, :, 8], mom[:, b.slot2, :, 7], epses[:, :], ALU.add)\
                        .then_inc(s_bve, 1)
                    wait(pool, s_bve, b.count(plus=1))
                    G.tensor_tensor(mom[:, b.slot2, :, 9], mom[:, b.slot2, :, 8], halves[:, :], ALU.pow)\
                        .then_inc(s_brd, 1)

            in_last_phase(pool, period)



        s_verdict = sem("verdict_parts")
        s_vsum = sem("verdict_summed")
        s_flag = sem("flag_ready")
        s_gx = sem("general_x_loaded")
        s_ga = sem("general_adj_loaded")
        s_gd = sem("general_rows_loaded")
        s_gout = sem("general_out_stored")
        graph = Chain(sem("general_graph_stages"), GRAPH_STAGES, 1)
        pairs = Chain(sem("general_pair_stages"), PAIR_STAGES, N // 4)
        rows3 = Chain(sem("general_row_stages"), ROW_STAGES, N // 4)

        used = [0]

        def room(cols):
            used[0] += cols
            assert used[0] <= 2 * 4 * TILES * N
            return space[:, used[0] - cols:used[0]]

        g_x = [room(F) for _ in range(5)]
        g_adj, g_adjT, g_xT, g_dst0 = (room(N) for _ in range(4))
        g_h = room(F + 1)
        g_score, g_edge, g_masked, g_prob, g_probT = (room(N) for _ in range(5))
        g_norm, g_mix, g_act, g_sum = (room(F) for _ in range(4))
        g_small = room(64)
        g_gl, g_gr, g_grn = (room(N) for _ in range(3))
        g_pair, g_pairL = room(4 * N), room(4 * N)
        g_e, g_e2 = room(H * N), room(H * N)
        g_none = room(N)
        g_sgn = room(H)
        g_d, g_dif, g_rad, g_z, g_y, g_w = (room(4 * N) for _ in range(6))
        g_turn, g_whole, g_cut = (room(4 * N) for _ in range(3))
        g_yT, g_agg = room(N), room(N)
        g_bias = room(1)

        def four(ap):
            return ap.rearrange("p (q j) -> p q j", j=N)

        def general_sync(sp):
            every_row = adj.rearrange("g i j -> (g i) j")
            with sp.Fori(0, B) as g:
                sp.dma_start(g_x[0], x[bass.ds(g, 1)].rearrange("a n f -> (a n) f")).then_inc(s_gx, 16)
                sp.dma_start(g_adj, adj[bass.ds(g, 1)].rearrange("a n f -> (a n) f")).then_inc(s_ga, 16)
                with sp.Fori(0, N // 4) as i:
                    four_rows = every_row[bass.ds(N * g + 4 * i, 4)].rearrange("(a q) j -> a q j", a=1)
                    sp.wait_ge(rows3.semaphore, rows3.after("start", g, i))
                    sp.dma_start(four(g_d), four_rows.to_broadcast([N, 4, N])).then_inc(s_gd, 16)
                sp.wait_ge(graph.semaphore, graph.after("layer3", g))
                sp.dma_start(out[bass.ds(g, 1)].rearrange("a n f -> (a n) f"), g_x[4]).then_inc(s_gout, 16)
                sp.wait_ge(s_gout, 16 * g + 16)
                sp.sem_inc(graph.semaphore, 1)

        def general_tensor(pe):
            mm = nc.tensor.matmul
            turn = nc.tensor.transpose
            done = graph.semaphore
            with pe.Fori(0, B) as g:
                pe.wait_ge(s_gx, 16 * g + 16)
                pe.wait_ge(s_ga, 16 * g + 16)
                pe.wait_ge(done, graph.after("start", g))
                for layer, weight in ((0, w0x), (1, w1x)):
                    if layer:
                        pe.wait_ge(done, graph.after("layer0", g))
                    turn(X1[:, 0:N], g_adj, ident[:, :])
                    turn(X0[:, 0:N], g_x[layer], ident[:, :]).then_inc(done, 1)
                    pe.wait_ge(done, graph.after(f"turned{layer}_kept", g))
                    mm(X0[:, 0:F], g_xT, weight[:, 0:F], start=True, stop=True)
                    mm(X0[:, F:F + 1], g_xT, wcol[:, 2 * layer:2 * layer + 1], start=True, stop=True)
                    mm(X0[:, 2 * F:2 * F + N], (g_dst0, dst1[:, :])[layer], g_xT, start=True, stop=True)\
                        .then_inc(done, 1)
                    pe.wait_ge(done, graph.after(f"probs{layer}", g))
                    turn(X2[:, 0:N], g_prob, ident[:, :]).then_inc(done, 1)
                    pe.wait_ge(done, graph.after(f"probsT{layer}_kept", g))
                    mm(X0[:, 0:F], g_probT, g_h[:, 0:F], start=True, stop=True)
                    mm(X0[:, F:2 * F], g_adjT, g_h[:, 0:F], start=True, stop=True).then_inc(done, 1)
                pe.wait_ge(done, graph.after("layer1", g))
                turn(X0[:, 0:N], g_x[2], ident[:, :]).then_inc(done, 1)
                pe.wait_ge(done, graph.after("turned2_kept", g))
                mm(X0[:, 0:N], wlT[:, :], g_xT, start=True, stop=True)
                mm(X0[:, N:2 * N], wrT[:, :], g_xT, start=True, stop=True)
                mm(X0[:, 2 * N:3 * N], g_xT, wrnT[:, :], start=True, stop=True).then_inc(done, 1)
                with pe.Fori(0, N // 4) as i:
                    pe.wait_ge(pairs.semaphore, pairs.after("lrelu", g, i))
                    for k in range(4):
                        ins = mm(X1[:, k * H:(k + 1) * H], g_pairL[:, k * N:(k + 1) * N], g_sgn,
                                 start=True, stop=True)
                    ins.then_inc(pairs.semaphore, 1)
                pe.wait_ge(done, graph.after("pairs", g))
                for h in range(H):
                    ins = turn((X0, X1)[h // 4][:, h % 4 * N:(h % 4 + 1) * N],
                               g_e.rearrange("p (i h) -> p i h", h=H)[:, :, h], ident[:, :])
                ins.then_inc(done, 1)
                pe.wait_ge(done, graph.after("sums2", g))
                for h in range(H):
                    ins = turn((X0, X1)[h // 4][:, h % 4 * N:(h % 4 + 1) * N], g_e2[:, h * N:(h + 1) * N],
                               ident[:, :])
                ins.then_inc(done, 1)
                pe.wait_ge(done, graph.after("probsT2_kept", g))
                for h in range(H):
                    ins = mm(X2[:, h * FH:(h + 1) * FH], g_e[:, h * N:(h + 1) * N], g_grn[:, h * FH:(h + 1) * FH],
                             start=True, stop=True)
                ins.then_inc(done, 1)
                pe.wait_ge(done, graph.after("layer2", g))
                turn(X0[:, 0:N], g_x[3], ident[:, :]).then_inc(done, 1)
                pe.wait_ge(done, graph.after("turned3_kept", g))
                mm(X0[:, 0:N], win[:, :], g_xT, start=True, stop=True).then_inc(done, 1)
                with pe.Fori(0, N // 4) as i:
                    pe.wait_ge(rows3.semaphore, rows3.after("radial", g, i))
                    mm(X1[:, :], w1f[:, :], g_rad[0:R, :], start=True, stop=True).then_inc(rows3.semaphore, 1)
                    pe.wait_ge(rows3.semaphore, rows3.after("ssp", g, i))
                    mm(X2[:, :], w2f[:, :], g_w, start=True, stop=True).then_inc(rows3.semaphore, 1)
                pe.wait_ge(done, graph.after("rows", g))
                mm(X0[:, 0:N], ow1s[:, :], g_agg, start=True, stop=True).then_inc(done, 1)
                pe.wait_ge(done, graph.after("softplus3", g))
                mm(X2[:, 0:F], ones[0:1, :], brow[0:1, 0, :], start=True, stop=False)
                mm(X2[:, 0:F], g_act, ow2s[:, :], start=False, stop=True).then_inc(done, 1)

        def general_scalar(act):
            A = nc.scalar.activation
            done = graph.semaphore
            with act.Fori(0, B) as g:
                for layer in range(2):
                    act.wait_ge(done, graph.after(f"turned{layer}", g))
                    A(g_adjT, X1[:, 0:N], ACT.Copy)
                    A(g_xT, X0[:, 0:N], ACT.Copy).then_inc(done, 1)
                    act.wait_ge(done, graph.after(f"h{layer}", g))
                    A(g_score, X0[:, 2 * F:2 * F + N], (ACT.Tanh, ACT.Identity)[layer], bias=g_h[:, F:F + 1])\
                        .then_inc(done, 1)
                    act.wait_ge(done, graph.after(f"max{layer}", g))
                    A(g_prob, g_masked, ACT.Exp, bias=g_small[:, 0:1], accum_out=g_small[:, 1:2]).then_inc(done, 1)
                    act.wait_ge(done, graph.after(f"probsT{layer}", g))
                    A(g_probT, X2[:, 0:N], ACT.Copy).then_inc(done, 1)
                act.wait_ge(done, graph.after("turned2", g))
                A(g_xT, X0[:, 0:N], ACT.Copy).then_inc(done, 1)
                act.wait_ge(done, graph.after("projected2", g))
                A(g_gl, X0[:, 0:N], ACT.Copy)
                A(g_gr, X0[:, N:2 * N], ACT.Copy)
                A(g_grn, X0[:, 2 * N:3 * N], ACT.Copy).then_inc(done, 1)
                with act.Fori(0, N // 4) as i:
                    act.wait_ge(pairs.semaphore, pairs.after("summed", g, i))
                    A(g_e[:, bass.ds(4 * H * i, 4 * H)], X1[:, 0:4 * H], ACT.Copy).then_inc(pairs.semaphore, 1)
                act.wait_ge(done, graph.after("shifted2", g))
                A(g_e, g_e2, ACT.Exp).then_inc(done, 1)
                act.wait_ge(done, graph.after("probsT2", g))
                A(g_e[:, 0:4 * N], X0[:, :], ACT.Copy)
                A(g_e[:, 4 * N:8 * N], X1[:, :], ACT.Copy).then_inc(done, 1)
                act.wait_ge(done, graph.after("turned3", g))
                A(g_xT, X0[:, 0:N], ACT.Copy).then_inc(done, 1)
                act.wait_ge(done, graph.after("projected3", g))
                A(g_yT, X0[:, 0:N], ACT.Copy).then_inc(done, 1)
                with act.Fori(0, N // 4) as i:
                    act.wait_ge(rows3.semaphore, rows3.after("rest", g, i))
                    A(g_rad[0:R, :], g_dif[0:R, :], ACT.Exp).then_inc(rows3.semaphore, 1)
                    act.wait_ge(rows3.semaphore, rows3.after("bias", g, i))
                    A(g_y, g_z, ACT.Abs).then_inc(rows3.semaphore, 1)
                    act.wait_ge(rows3.semaphore, rows3.after("abs", g, i))
                    A(g_y, g_y, ACT.Exp, scale=-1.0).then_inc(rows3.semaphore, 1)
                    act.wait_ge(rows3.semaphore, rows3.after("exp", g, i))
                    A(g_y, g_y, ACT.Ln, bias=1.0).then_inc(rows3.semaphore, 1)
                    act.wait_ge(rows3.semaphore, rows3.after("filter", g, i))
                    A(g_turn, g_turn, ACT.Abs).then_inc(rows3.semaphore, 1)
                    act.wait_ge(rows3.semaphore, rows3.after("size", g, i))
                    A(g_turn, g_turn, ACT.Sin, scale=-2.0 * math.pi, bias=g_bias[:, 0:1]).then_inc(rows3.semaphore, 1)
                act.wait_ge(done, graph.after("bias3", g))
                A(g_mix, g_norm, ACT.Abs).then_inc(done, 1)
                act.wait_ge(done, graph.after("abs3", g))
                A(g_mix, g_mix, ACT.Exp, scale=-1.0).then_inc(done, 1)
                act.wait_ge(done, graph.after("exp3", g))
                A(g_mix, g_mix, ACT.Ln, bias=1.0).then_inc(done, 1)

        def general_pool(pool):
            G = nc.gpsimd
            done = graph.semaphore
            with pool.Fori(0, B) as g:
                for layer in range(4):
                    pool.wait_ge(done, graph.after(f"var{layer}", g))
                    G.tensor_tensor(g_small[:, 10:11], g_small[:, 9:10], epses[:, 0:1], ALU.add).then_inc(done, 1)
                    pool.wait_ge(done, graph.after(f"vareps{layer}", g))
                    G.tensor_tensor(g_small[:, 11:12], g_small[:, 10:11], halves[:, 0:1], ALU.pow).then_inc(done, 1)

        def general_vector(dve):
            V = nc.vector
            done = graph.semaphore

            def normalize(g, layer):
                dve.wait_ge(done, graph.after(f"added{layer}", g))
                V.bn_stats(g_small[:, 2:8], g_sum).then_inc(done, 1)
                dve.wait_ge(done, graph.after(f"moments{layer}", g))
                dve.sem_inc(done, 1)
                V.bn_aggr(g_small[:, 8:10], g_small[:, 2:8]).then_inc(done, 1)
                dve.wait_ge(done, graph.after(f"rstd{layer}", g))
                V.tensor_scalar(g_x[layer + 1], g_sum, g_small[:, 8:9], g_small[:, 11:12],
                                ALU.subtract, ALU.mult).then_inc(done, 1)

            dve.wait_ge(s_gx, 16)
            V.memset(g_bias[:, 0:1], math.pi / 2)
            V.tensor_copy(g_dst0, bcast(wcol[:, 1:2], [F, N]))
            V.tensor_scalar(g_sgn, sgn8[:, :], 1.0 / (1.0 - SLOPE), None, ALU.mult).then_inc(s_own, 1)
            dve.wait_ge(s_own, 11)
            with dve.Fori(0, B) as g:
                dve.wait_ge(s_gx, 16 * g + 16)
                dve.wait_ge(s_ga, 16 * g + 16)
                V.tensor_scalar(g_edge, g_adj, 0.0, None, ALU.is_gt)
                V.tensor_scalar(g_none, g_adj, 0.0, None, ALU.is_equal).then_inc(done, 1)
                for layer in range(2):
                    dve.wait_ge(done, graph.after(f"projected{layer}", g))
                    V.tensor_copy(g_h, X0[:, 0:F + 1]).then_inc(done, 1)
                    dve.wait_ge(done, graph.after(f"scores{layer}", g))
                    if layer == 0:
                        V.tensor_tensor(g_prob, g_score, g_edge, ALU.mult)
                        V.tensor_scalar(g_mix, g_edge, 1.0e15, -1.0e15, ALU.mult, ALU.add).then_inc(done, 1)
                        dve.wait_ge(done, graph.after("edges0", g))
                        V.tensor_tensor(g_masked, g_prob, g_mix, ALU.add).then_inc(done, 1)
                        dve.wait_ge(done, graph.after("masked0", g))
                    else:
                        V.scalar_tensor_tensor(g_masked, g_score, SLOPE, g_score, ALU.mult, ALU.max)\
                            .then_inc(done, 1)
                        dve.wait_ge(done, graph.after("lrelu1", g))
                    V.tensor_reduce(g_small[:, 0:1], g_masked, X, ALU.max, negate=True).then_inc(done, 1)
                    dve.wait_ge(done, graph.after(f"attended{layer}", g))
                    V.tensor_reduce(g_small[:, 13:14], g_adjT, X, ALU.add)
                    V.reciprocal(g_small[:, 12:13], g_small[:, 1:2]).then_inc(done, 1)
                    dve.wait_ge(done, graph.after(f"recip{layer}", g))
                    if layer == 0:
                        V.tensor_scalar(g_small[:, 14:15], g_small[:, 13:14], 0.0, 1.0, ALU.is_equal, ALU.add)
                        V.tensor_scalar(g_small[:, 15:16], g_small[:, 13:14], 0.0, g_small[:, 12:13],
                                        ALU.not_equal, ALU.mult).then_inc(done, 1)
                        dve.wait_ge(done, graph.after("weight0", g))
                        V.tensor_scalar(g_norm, X0[:, 0:F], g_small[:, 15:16], None, ALU.mult).then_inc(done, 1)
                        dve.wait_ge(done, graph.after("norm0", g))
                        V.scalar_tensor_tensor(g_sum, g_x[0], g_small[:, 14:15], g_norm, ALU.mult, ALU.add)\
                            .then_inc(done, 1)
                    else:
                        V.tensor_scalar(g_norm, X0[:, 0:F], g_small[:, 12:13], None, ALU.mult).then_inc(done, 1)
                        dve.wait_ge(done, graph.after("norm1", g))
                        V.tensor_tensor(g_mix, g_norm, X0[:, F:2 * F], ALU.add).then_inc(done, 1)
                        dve.wait_ge(done, graph.after("mixed1", g))
                        V.scalar_tensor_tensor(g_act, g_mix, SLOPE, g_mix, ALU.mult, ALU.max).then_inc(done, 1)
                        dve.wait_ge(done, graph.after("act1", g))
                        V.tensor_tensor(g_sum, g_act, g_x[1], ALU.add).then_inc(done, 1)
                    normalize(g, layer)
                dve.wait_ge(done, graph.after("projected2_kept", g))
                dve.sem_inc(pairs.semaphore, 1)
                with dve.Fori(0, N // 4) as i:
                    dve.wait_ge(pairs.semaphore, pairs.after("start", g, i))
                    V.tensor_tensor(four(g_pair), bcast(g_gl.rearrange("p (a j) -> p a j", a=1), [F, 4, N]),
                                    bcast(g_gr[:, bass.ds(4 * i, 4)].rearrange("p (a k) -> p a k", k=1), [F, 4, N]),
                                    ALU.add).then_inc(pairs.semaphore, 1)
                    dve.wait_ge(pairs.semaphore, pairs.after("added", g, i))
                    V.scalar_tensor_tensor(g_pairL, g_pair, SLOPE, g_pair, ALU.mult, ALU.max)\
                        .then_inc(pairs.semaphore, 1)
                dve.wait_ge(pairs.semaphore, pairs.after("kept", g, N // 4 - 1))
                dve.sem_inc(done, 1)
                dve.wait_ge(done, graph.after("turned_scores2", g))
                for k in range(2):
                    V.tensor_tensor(four(g_e2[:, k * 4 * N:(k + 1) * 4 * N]), four((X0, X1)[k][:, :]),
                                    bcast(g_adj.rearrange("p (a j) -> p a j", a=1), [N, 4, N]), ALU.mult)
                V.tensor_scalar(g_mix, g_none, -MASKED, None, ALU.mult).then_inc(done, 1)
                dve.wait_ge(done, graph.after("weighed2", g))
                V.tensor_tensor(four(g_e), four(g_e2), bcast(g_mix.rearrange("p (a j) -> p a j", a=1), [N, H, N]),
                                ALU.add).then_inc(done, 1)
                dve.wait_ge(done, graph.after("masked2", g))
                V.tensor_scalar(g_mix, g_none, -1.0, 1.0, ALU.mult, ALU.add)
                V.tensor_reduce(g_small[:, 16:16 + H], four(g_e), X, ALU.max, negate=True).then_inc(done, 1)
                dve.wait_ge(done, graph.after("max2", g))
                V.tensor_tensor(four(g_e2), four(g_e),
                                bcast(g_small[:, 16:16 + H].rearrange("p (h k) -> p h k", k=1), [N, H, N]),
                                ALU.add).then_inc(done, 1)
                dve.wait_ge(done, graph.after("exps2", g))
                V.tensor_tensor(four(g_e2), four(g_e), bcast(g_mix.rearrange("p (a j) -> p a j", a=1), [N, H, N]),
                                ALU.mult).then_inc(done, 1)
                dve.wait_ge(done, graph.after("edges2", g))
                V.tensor_reduce(g_small[:, 24:24 + H], four(g_e2), X, ALU.add).then_inc(done, 1)
                dve.wait_ge(done, graph.after("attended2", g))
                V.reciprocal(g_small[:, 32:32 + H], g_small[:, 24:24 + H]).then_inc(done, 1)
                dve.wait_ge(done, graph.after("recips2", g))
                V.tensor_tensor(g_norm.rearrange("p (h f) -> p h f", h=H),
                                X2[:, 0:F].rearrange("p (h f) -> p h f", h=H),
                                bcast(g_small[:, 32:32 + H].rearrange("p (h k) -> p h k", k=1), [N, H, FH]),
                                ALU.mult).then_inc(done, 1)
                dve.wait_ge(done, graph.after("norm2", g))
                V.scalar_tensor_tensor(g_act, g_norm, SLOPE, g_norm, ALU.mult, ALU.max).then_inc(done, 1)
                dve.wait_ge(done, graph.after("act2", g))
                V.tensor_tensor(g_sum, g_act, g_x[2], ALU.add).then_inc(done, 1)
                normalize(g, 2)
                dve.wait_ge(done, graph.after("projected3_kept", g))
                dve.sem_inc(rows3.semaphore, 1)
                with dve.Fori(0, N // 4) as i:
                    step = rows3.semaphore
                    dve.wait_ge(s_gd, (16 * N // 4) * g + 16 * i + 16)
                    dve.wait_ge(step, rows3.after("start", g, i))
                    V.tensor_scalar(g_dif[0:R, :], g_d[0:R, :], radial[:, 1:2], None, ALU.subtract)
                    V.tensor_scalar(g_turn, g_d, 0.5 / CUTOFF, None, ALU.mult)
                    V.tensor_scalar(g_cut, g_d, CUTOFF, None, ALU.is_lt).then_inc(step, 1)
                    dve.wait_ge(step, rows3.after("offset", g, i))
                    V.tensor_tensor(g_dif[0:R, :], g_dif[0:R, :], g_dif[0:R, :], ALU.mult)
                    V.tensor_scalar(g_whole, g_turn, ROUNDER, None, ALU.add).then_inc(step, 1)
                    dve.wait_ge(step, rows3.after("squares", g, i))
                    V.tensor_scalar(g_dif[0:R, :], g_dif[0:R, :], radial[:, 3:4], -0.5, ALU.mult, ALU.mult)
                    V.tensor_scalar(g_whole, g_whole, -ROUNDER, None, ALU.add).then_inc(step, 1)
                    dve.wait_ge(step, rows3.after("exponents", g, i))
                    V.tensor_tensor(g_turn, g_turn, g_whole, ALU.subtract).then_inc(step, 1)
                    dve.wait_ge(step, rows3.after("hidden", g, i))
                    V.tensor_scalar(g_z, X1[:, :], vec[:, 4:5], None, ALU.add).then_inc(step, 1)
                    dve.wait_ge(step, rows3.after("ln", g, i))
                    V.scalar_tensor_tensor(g_z, g_z, 0.0, g_y, ALU.max, ALU.add).then_inc(step, 1)
                    dve.wait_ge(step, rows3.after("softplus", g, i))
                    V.tensor_scalar(g_w, g_z, -LOG2, None, ALU.add).then_inc(step, 1)
                    dve.wait_ge(step, rows3.after("cosine", g, i))
                    V.tensor_scalar(g_turn, g_turn, 0.5, 0.5, ALU.mult, ALU.add).then_inc(step, 1)
                    dve.wait_ge(step, rows3.after("raised", g, i))
                    V.tensor_tensor(g_cut, g_turn, g_cut, ALU.mult).then_inc(step, 1)
                    dve.wait_ge(step, rows3.after("cut", g, i))
                    V.scalar_tensor_tensor(g_z, X2[:, :], vec[:, 5:6], g_cut, ALU.add, ALU.mult).then_inc(step, 1)
                    dve.wait_ge(step, rows3.after("weighed", g, i))
                    V.tensor_tensor(four(g_y), four(g_z), bcast(g_yT.rearrange("p (a j) -> p a j", a=1), [F, 4, N]),
                                    ALU.mult).then_inc(step, 1)
                    dve.wait_ge(step, rows3.after("messages", g, i))
                    V.tensor_reduce(g_agg[:, bass.ds(4 * i, 4)], four(g_y), X, ALU.add).then_inc(step, 1)
                dve.wait_ge(rows3.semaphore, rows3.after("kept", g, N // 4 - 1))
                dve.sem_inc(done, 1)
                dve.wait_ge(done, graph.after("hidden3", g))
                V.tensor_scalar(g_norm, X0[:, 0:N], vec[:, 6:7], None, ALU.add).then_inc(done, 1)
                dve.wait_ge(done, graph.after("ln3", g))
                V.scalar_tensor_tensor(g_act, g_norm, 0.0, g_mix, ALU.max, ALU.add).then_inc(done, 1)
                dve.wait_ge(done, graph.after("output3", g))
                V.tensor_tensor(g_sum, X2[:, 0:F], g_x[3], ALU.add).then_inc(done, 1)
                normalize(g, 3)

        def find_verdict(dve):
            V = nc.vector
            dve.wait_ge(s_ck2, B)
            dve.wait_ge(s_lc, B)
            dve.wait_ge(s_xaC, B)
            V.tensor_reduce(verdict[:, 0:1], chk_all[:, :], X, ALU.max)
            V.tensor_reduce(verdict[:, 1:2], sum_all[:, :], X, ALU.min)
            V.tensor_reduce(verdict[:, 2:3], deg_all[:, :], X, ALU.min).then_inc(s_verdict, 1)
            dve.wait_ge(s_verdict, 1)
            V.tensor_scalar(verdict[:, 3:4], verdict[:, 0:1], 0.0, None, ALU.is_gt)
            V.tensor_scalar(verdict[:, 4:6], verdict[:, 1:3], 0.0, None, ALU.is_le).then_inc(s_verdict, 1)
            dve.wait_ge(s_vsum, 1)
            V.tensor_reduce(verdict[0:1, 6:7], X0[0:1, 0:3], X, ALU.add).then_inc(s_verdict, 1)
            dve.wait_ge(s_verdict, 3)
            V.tensor_copy(flag[:, :], verdict[0:1, 6:7]).then_inc(s_flag, 1)

        def sum_verdict(pe):
            pe.wait_ge(s_verdict, 2)
            nc.tensor.matmul(X0[0:1, 0:3], ones[:, 0:1], verdict[:, 3:6], start=True, stop=True).then_inc(s_vsum, 1)

        def where_needed(engine, general):
            engine.wait_ge(s_flag, 1)
            count = engine.value_load(flag[0:1, 0:1])
            with engine.If(count > 0):
                general(engine)

        LOADS = 0
        weights = [(ident[:, :], ident_in), (heads[:, :], heads_in), (w0x[:, 0:F], W0), (w1x[:, 0:F], W1),
                   (raw[:, 0, :], W_l), (raw[:, 1, :], W_r), (win[:, :], w_in2f), (w1f[:, :], fw1),
                   (w2f[:, :], fw2), (ow1s[:, :], ow1), (ow2s[:, :], ow2),
                   (vec[:, 0:1], a0.rearrange("(f k) -> f k", k=1)[0:F]),
                   (vec[:, 1:2], a0.rearrange("(f k) -> f k", k=1)[F:2 * F]),
                   (vec[:, 2:3], a1.rearrange("(f k) -> f k", k=1)[0:F]),
                   (vec[:, 3:4], a1.rearrange("(f k) -> f k", k=1)[F:2 * F]),
                   (vec[:, 4:5], fb1.rearrange("(f k) -> f k", k=1)),
                   (vec[:, 5:6], fb2.rearrange("(f k) -> f k", k=1)),
                   (vec[:, 6:7], ob1.rearrange("(f k) -> f k", k=1)),
                   (radial[:, 0:1], widths.rearrange("(f k) -> f k", k=1)),
                   (radial[:, 1:2], offsets.rearrange("(f k) -> f k", k=1)),
                   (brow[:, 4, :], ob2.rearrange("(k f) -> k f", k=1))]
        weights += [(vec[FH * h:FH * (h + 1), 7:8], w_attn.rearrange("(f k) -> f k", k=1)) for h in range(H)]
        LOADS = len(weights)

        def load_first(sp, g):
            wait(sp, s_sm0, g.count(plus=-3), B)
            sp.dma_start(xin[:, g.slot4, :], g.pick(x)).then_inc(s_x[g.slot4], 16)
            wait(sp, s_ck, g.count(plus=-3), B)
            wait(sp, s_xaT, g.count(plus=-3), B)
            sp.dma_start(adj_a[:, g.slot4, :], g.pick(adj)).then_inc(s_aa[g.slot4], 16)

        @block.sync
        def _(sp):
            for to, source in weights:
                sp.dma_start(to, source).then_inc(s_w, 16)

            def period(fours, u):
                g = Item(fours, u)
                if g.there():
                    load_first(sp, g)
                g = Item(fours, u - 1)
                if g.there():
                    wait(sp, s_x3T, g.count(plus=-3), B)
                    wait(sp, s_mb, g.count(plus=-3), B)
                    sp.dma_start(adj_b[:, g.slot4, :], g.pick(adj)).then_inc(s_ab[g.slot4], 16)
                g = Item(fours, u - 4)
                if g.there():
                    wait(sp, s_x3, g.count(plus=1))
                    sp.dma_start(x3_all[:, g.columns()], x3[:, g.slot2, :]).then_inc(s_x3k[g.slot2], 16)

            for u in range(RING):
                period(0, u)
            with sp.Fori(1, B // RING) as fours:
                for u in range(RING):
                    period(fours, u)
            for u in range(LAST_STAGE):
                period(B // RING, u)
            for k in range(2):
                sp.wait_ge(s_x3k[k], 16 * B // 2)
            last_phase_sync(sp)
            where_needed(sp, general_sync)

        @block.tensor
        def _(pe):
            mm = nc.tensor.matmul
            pe.wait_ge(s_w, 16 * LOADS)
            nc.tensor.transpose(X0[:, 0:F], w0x[:, 0:F], ident[:, :])
            nc.tensor.transpose(X0[:, F:2 * F], w1x[:, 0:F], ident[:, :]).then_inc(s_wT, 1)
            pe.wait_ge(s_wTC, 1)
            mm(X1[:, 0:2], raw[:, 2, :], vec[:, 0:2], start=True, stop=True)
            mm(X1[:, 2:4], raw[:, 3, :], vec[:, 2:4], start=True, stop=True).then_inc(s_wa, 1)
            pe.wait_ge(s_scl, 1)
            nc.tensor.transpose(X2[:, 0:F], raw[:, 4, :], ident[:, :])
            nc.tensor.transpose(X2[:, F:2 * F], raw[:, 5, :], ident[:, :])
            nc.tensor.transpose(X2[:, 2 * F:3 * F], raw[:, 1, :], ident[:, :]).then_inc(s_wlr, 1)
            pe.wait_ge(s_rad, 1)
            pe.wait_ge(s_ones, 1)
            mm(T[:, 0:2], w1f[:, :], radial[:, 6:8], start=True, stop=True)
            mm(T[0:1, F:2 * F], ones[:, 0:1], ow2s[:, :], start=True, stop=True).then_inc(s_hid, 1)
            pe.wait_ge(s_ssp, 1)
            mm(T[:, 2:4], w2f[:, :], filt[:, 6:8], start=True, stop=True).then_inc(s_fil, 1)
            pe.wait_ge(s_ready, 1)

            def pair_sums(g, step):
                half, t = step // 4, step % 4
                wait(pe, s_zv, g.count(STEPS, step + 1))
                wait(pe, s_za, g.count(STEPS, step + 1))
                wait(pe, s_zp, g.count(STEPS, step + 1))
                if t == 0:
                    wait(pe, s_e2, g.count(2, half - 1))
                for c in range(4):
                    last = mm(E[half][32 * c:32 * c + 32, :], ssum[:, t, :],
                              Z[:, half, t, 4 * c:4 * c + 4, :].rearrange("p q j -> p (q j)"),
                              start=(t == 0), stop=False, skip_group_check=True)
                last.then_inc(s_zu, 1)
                if t < 3:
                    return
                if half == 0:
                    wait(pe, s_mb, g.count(plus=1))
                mm(E[half][:, :].rearrange("p (q j) -> p q j", q=4), slin[:, :, :].rearrange("p m h -> p (m h)"),
                   bcast(gl[:, g.slot2:g.slot2 + 1, :], [F, 4, N]), start=False, stop=False, skip_group_check=True)
                for q in range(4):
                    last = mm(E[half][:, q * N:(q + 1) * N],
                              rows[:, half * 4 + q, :, :].rearrange("p m h -> p (m h)"), maskb[:, g.slot2, :],
                              start=False, stop=(q == 3), skip_group_check=True)
                last.then_inc(s_sc, 1)

            def transpose_probs(g, half):
                wait(pe, s_e2, g.count(2, half + 1))
                wait(pe, s_pC, g.count(2, half))
                for q in range(4):
                    last = nc.tensor.transpose(T[:, q * N:(q + 1) * N], prob2[:, half, q, :], ident[:, :])
                last.then_inc(s_pT, 1)

            def period(fours, u):
                a, b, c, d, e = (Item(fours, u - k) for k in range(5))
                if a.there():
                    pe.wait_ge(s_x[a.slot4], a.loads())
                    pe.wait_ge(s_aa[a.slot4], a.loads())
                    wait(pe, s_grx, a.count(plus=-1))
                    nc.tensor.transpose(X0[:, 0:N], xin[:, a.slot4, :], ident[:, :])
                    nc.tensor.transpose(X0[:, N:2 * N], adj_a[:, a.slot4, :], ident[:, :]).then_inc(s_xaT, 1)
                if e.there():
                    wait(pe, s_x3C, e.count(plus=1))
                    mm(X2[:, 0:F], xa3[:, e.slot2, 0:N], win[:, :], start=True, stop=True).then_inc(s_y3, 1)
                if d.there():
                    pair_sums(d, 7)
                if a.there():
                    wait(pe, s_xaC, a.count(plus=1))
                    mm(X0[:, 0:F + 1], xa[:, a.slot2, 0:N], w0x[:, :], start=True, stop=True)
                    mm(X0[:, 256:384], src0[:, :], xa[:, a.slot2, 0:N], start=True, stop=True).then_inc(s_p0, 1)
                if b.there():
                    wait(pe, s_e1, b.count(plus=1))
                    mm(X1[:, 0:F + 1], prob1[:, b.slot2, :], h1[:, b.slot2, 0:F + 1], start=True, stop=True)
                    mm(X1[:, 256:384], xa[:, b.slot2, N:2 * N], h1[:, b.slot2, 1:F + 1],
                       start=True, stop=True).then_inc(s_at1, 1)
                if e.there():
                    wait(pe, s_y3C, e.count(plus=1))
                    mm(X2[:, 128:257], y3[:, e.slot2, :], xa3[:, e.slot2, N:2 * N + 1],
                       start=True, stop=True).then_inc(s_ag3, 1)
                if c.there():
                    pair_sums(c, 0)
                if c.there():
                    pair_sums(c, 1)
                if a.there():
                    wait(pe, s_pr0, a.count(plus=1))
                    mm(X0[:, 0:F + 1], prob0[:, a.slot2, :], h0[:, a.slot2, 0:F + 1],
                       start=True, stop=True).then_inc(s_at0, 1)
                if d.there():
                    transpose_probs(d, 1)
                if c.there():
                    pair_sums(c, 2)
                if b.there():
                    wait(pe, s_x2, b.count(plus=1))
                    wait(pe, s_sm0, b.count(plus=2), B)
                    nc.tensor.transpose(X0[:, 0:N], x2[:, b.slot4, :], ident[:, :]).then_inc(s_x2T, 1)
                if d.there():
                    wait(pe, s_pC, d.count(2, 2))
                    wait(pe, s_agC, d.count())
                    for h in range(H):
                        last = mm(X2[:, h * HE:(h + 1) * HE],
                                  pT[:, :, :, :, :].rearrange("p c q a (t h) -> p (c q a t) h", h=H)[:, :, h],
                                  grx[:, d.slot2, h, :], start=True, stop=True)
                    last.then_inc(s_at2, 1)
                if c.there():
                    pair_sums(c, 3)
                if a.there():
                    wait(pe, s_x1, a.count(plus=1))
                    wait(pe, s_mix1, a.count())
                    nc.tensor.transpose(X1[:, 0:N], x1[:, a.slot2, :], ident[:, :]).then_inc(s_x1T, 1)
                if b.there():
                    wait(pe, s_x2C, b.count(plus=1))
                    wait(pe, s_zv, b.count(STEPS, -STEPS))
                    mm(GL[b.slot2][:, 0:N], wlT[:, :], x2T[:, b.slot2, :], start=True, stop=True)
                    mm(X0[:, 0:N], wrT[:, :], x2T[:, b.slot2, :], start=True, stop=True)
                    mm(X0[:, N:2 * N], x2T[:, b.slot2, :], wrnT[:, :], start=True, stop=True).then_inc(s_p2, 1)
                if c.there():
                    pair_sums(c, 4)
                if a.there():
                    wait(pe, s_x1C, a.count(plus=1))
                    mm(X1[:, 0:F + 1], x1T[:, a.slot2, :], w1x[:, :], start=True, stop=True)
                    mm(X1[:, 256:384], src1[:, :], x1T[:, a.slot2, :], start=True, stop=True)
                    wait(pe, s_nm2, a.count(plus=-2))
                    mm(X2[:, 384:512], dst1[:, :], x1T[:, a.slot2, :], start=True, stop=True).then_inc(s_p1, 1)
                if c.there():
                    pair_sums(c, 5)
                if d.there():
                    wait(pe, s_x3, d.count(plus=1))
                    pe.wait_ge(s_ab[d.slot4], d.loads())
                    wait(pe, s_mx1, d.count(plus=4), B)
                    nc.tensor.transpose(X2[:, 0:N], x3[:, d.slot2, :], ident[:, :])
                    nc.tensor.transpose(X2[:, N:2 * N], adj_b[:, d.slot4, :], ident[:, :]).then_inc(s_x3T, 1)
                if c.there():
                    transpose_probs(c, 0)
                    pair_sums(c, 6)

            for u in range(RING):
                period(0, u)
            with pe.Fori(1, B // RING) as fours:
                for u in range(RING):
                    period(fours, u)
            for u in range(LAST_STAGE + 1):
                period(B // RING, u)
            last_phase_tensor(pe)
            sum_verdict(pe)
            where_needed(pe, general_tensor)

        @block.scalar
        def _(act):
            A = nc.scalar.activation
            act.wait_ge(s_w, 16 * LOADS)
            act.wait_ge(s_rade, 1)
            A(radial[:, 6:8], radial[:, 4:6], ACT.Exp).then_inc(s_rad, 1)
            act.wait_ge(s_hidb, 1)
            A(filt[:, 2:4], filt[:, 0:2], ACT.Abs).then_inc(s_soft, 1)
            act.wait_ge(s_soft, 1)
            A(filt[:, 2:4], filt[:, 2:4], ACT.Exp, scale=-1.0).then_inc(s_soft, 1)
            act.wait_ge(s_soft, 2)
            A(filt[:, 4:6], filt[:, 2:4], ACT.Ln, bias=1.0).then_inc(s_soft, 1)
            act.wait_ge(s_ready, 1)

            def tiles(g, step):
                half, t = step // 4, step % 4
                wait(act, s_zu, g.count(STEPS, step + 1 - STEPS))
                for k in range(DVE_TILES[step], DVE_TILES[step] + ACT_TILES[step]):
                    i = 8 * k + step
                    A(Z[:, half, t, k, :], gl[:, g.slot2, :], ACT.Relu, bias=gr[:, g.slot2, i:i + 1])

            def finish_tiles(g, step):
                half, t = step // 4, step % 4
                first = DVE_TILES[step] + ACT_TILES[step]
                wait(act, s_zp, g.count(STEPS, step + 1))
                A(Z[:, half, t, first:TILES, :], Z[:, half, t, first:TILES, :], ACT.Relu).then_inc(s_za, 1)

            def exps(g, half):
                wait(act, s_mx2, g.count(2, half + 1))
                wait(act, s_pT, g.count(2, half - 1))
                for q in range(4):
                    ins = A(prob2[:, half, q, :], E[half][:, q * N:(q + 1) * N], ACT.Exp,
                            bias=negmax[:, g.slot2, half * 4 + q:half * 4 + q + 1])
                ins.then_inc(s_e2, 1)

            def copy_probs(g, half):
                wait(act, s_pT, g.count(2, half + 1))
                wait(act, s_at2, g.count())
                A(pT[:, :, :, half, :].rearrange("p c q k -> p q c k"),
                  T[:, :].rearrange("p (q c k) -> p q c k", q=4, c=4), ACT.Copy).then_inc(s_pC, 1)

            def period(fours, u):
                a, b, c, d, e = (Item(fours, u - k) for k in range(5))
                on = c.there()
                if d.there():
                    finish_tiles(d, 7)
                if on:
                    wait(act, s_gl, c.count(plus=1))
                    wait(act, s_gr, c.count(plus=1))
                    tiles(c, 0)
                if a.there():
                    wait(act, s_xaT, a.count(plus=1))
                    wait(act, s_p0, a.count(plus=-1))
                    wait(act, s_at1, a.count(plus=-1))
                    A(xa[:, a.slot2, 0:N], X0[:, 0:N], ACT.Copy)
                    A(xa[:, a.slot2, N:2 * N], X0[:, N:2 * N], ACT.Copy,
                      accum_out=deg_all[:, a.columns(1)]).then_inc(s_xaC, 1)
                if b.there():
                    wait(act, s_d1, b.count(plus=1))
                    A(prob1[:, b.slot2, :], dif1[:, b.slot2, :], ACT.Exp, scale=1.0 - SLOPE,
                      bias=small[:, b.slot2, 23:24]).then_inc(s_e1, 1)
                if e.there():
                    wait(act, s_y3, e.count(plus=1))
                    A(y3[:, e.slot2, :], X2[:, 0:F], ACT.Copy).then_inc(s_y3C, 1)
                if on:
                    finish_tiles(c, 0)
                    tiles(c, 1)
                if b.there():
                    wait(act, s_at1, b.count(plus=1))
                    A(nbr1[:, b.slot2, :], X1[:, 256:384], ACT.Copy).then_inc(s_nb1, 1)
                if a.there():
                    wait(act, s_p0, a.count(plus=1))
                    A(h0[:, a.slot2, 1:F + 2], X0[:, 0:F + 1], ACT.Copy).then_inc(s_h0, 1)
                if a.there():
                    wait(act, s_h0, a.count(plus=1))
                    A(tanh0[:, a.slot2, :], X0[:, 256:384], ACT.Tanh,
                      bias=h0[:, a.slot2, F + 1:F + 2]).then_inc(s_th, 1)
                if e.there():
                    wait(act, s_ag3, e.count(plus=1))
                    A(ysum[:, e.slot2, :], X2[:, 256:257], ACT.Copy, scale=filt[:, 8:9]).then_inc(s_ys, 1)
                if on:
                    finish_tiles(c, 1)
                    tiles(c, 2)
                if a.there():
                    wait(act, s_th, a.count(plus=1))
                    A(exp0[:, a.slot2, :], tanh0[:, a.slot2, :], ACT.Exp).then_inc(s_e0, 1)
                if e.there():
                    wait(act, s_ys, e.count(plus=1))
                    A(agg_all[:, e.columns()], X2[:, 128:256], ACT.Identity, scale=filt[:, 9:10],
                      bias=ysum[:, e.slot2, :]).then_inc(s_agC, 1)
                if d.there():
                    exps(d, 1)
                if on:
                    finish_tiles(c, 2)
                    tiles(c, 3)
                if d.there():
                    copy_probs(d, 1)
                if on:
                    finish_tiles(c, 3)
                    tiles(c, 4)
                if b.there():
                    wait(act, s_x2T, b.count(plus=1))
                    A(x2T[:, b.slot2, :], X0[:, 0:N], ACT.Copy).then_inc(s_x2C, 1)
                if on:
                    finish_tiles(c, 4)
                    tiles(c, 5)
                if b.there():
                    wait(act, s_p2, b.count(plus=1))
                    wait(act, s_sc, b.count(2, -2))
                    wait(act, s_zp, b.count(STEPS, -STEPS))
                    wait(act, s_zv, b.count(STEPS, -STEPS))
                    wait(act, s_at2, b.count(plus=-1))
                    A(gl[:, b.slot2, :], GL[b.slot2][:, 0:N], ACT.Copy).then_inc(s_gl, 1)
                    A(gr[:, b.slot2, :], X0[:, 0:N], ACT.Copy).then_inc(s_gr, 1)
                    A(ngr[:, b.slot2, :], X0[:, 0:N], ACT.Copy, scale=-1.0).then_inc(s_ngr, 1)
                    A(grx[:, b.slot2, :, 0:FH], X0[:, N:2 * N].rearrange("p (h f) -> p h f", h=H),
                      ACT.Copy).then_inc(s_grx, 1)
                if a.there():
                    wait(act, s_x1T, a.count(plus=1))
                    A(x1T[:, a.slot2, :], X1[:, 0:N], ACT.Copy).then_inc(s_x1C, 1)
                if on:
                    finish_tiles(c, 5)
                    tiles(c, 6)
                if a.there():
                    wait(act, s_p1, a.count(plus=1))
                    A(h1[:, a.slot2, 1:F + 2], X1[:, 0:F + 1], ACT.Copy).then_inc(s_h1, 1)
                if c.there():
                    exps(c, 0)
                if a.there():
                    wait(act, s_h1, a.count(plus=1))
                    A(relu1[:, a.slot2, :], X1[:, 256:384], ACT.Relu,
                      bias=h1[:, a.slot2, F + 1:F + 2]).then_inc(s_u1, 1)
                if on:
                    finish_tiles(c, 6)
                    tiles(c, 7)
                if a.there():
                    wait(act, s_mx1, a.count(plus=1))
                    A(max1[:, a.slot2, :], X1[:, 256:384], ACT.Relu,
                      bias=small[:, a.slot2, 20:21]).then_inc(s_m1, 1)
                if c.there():
                    copy_probs(c, 0)
                if d.there():
                    wait(act, s_x3T, d.count(plus=1))
                    wait(act, s_ag3, d.count(plus=-1))
                    A(xa3[:, d.slot2, 0:2 * N], X2[:, 0:2 * N], ACT.Copy).then_inc(s_x3C, 1)

            for u in range(RING):
                period(0, u)
            with act.Fori(1, B // RING) as fours:
                for u in range(RING):
                    period(fours, u)
            for u in range(LAST_STAGE + 1):
                period(B // RING, u)
            last_phase_scalar(act)
            where_needed(act, general_scalar)

        @block.vector
        def _(dve):
            V = nc.vector
            V.memset(ones[:, :], 1.0).then_inc(s_ones, 1)
            for k in range(2):
                V.memset(h0[:, k, 0:1], 1.0)
                V.memset(h1[:, k, 0:1], 1.0)
                V.memset(grx[:, k, :, FH:HE], 1.0)
                V.memset(xa3[:, k, 2 * N:2 * N + 1], 1.0)
            V.memset(ssum[:, :, :], 0.0).then_inc(s_ones, 1)
            dve.wait_ge(s_w, 16 * LOADS)
            dve.wait_ge(s_wT, 1)
            V.tensor_copy(raw[:, 2:4, :].rearrange("p k f -> p (k f)"), X0[:, 0:2 * F]).then_inc(s_wTC, 1)
            V.tensor_scalar(sgn[:, 0:1], vec[:, 7:8], 0.0, None, ALU.is_gt)
            V.tensor_scalar(sgn[:, 1:2], vec[:, 7:8], 0.0, None, ALU.is_lt).then_inc(s_own, 1)
            dve.wait_ge(s_own, 1)
            V.tensor_tensor(sgn[:, 2:3], sgn[:, 0:1], sgn[:, 1:2], ALU.subtract).then_inc(s_own, 1)
            dve.wait_ge(s_own, 2)
            V.scalar_tensor_tensor(sgn[:, 3:4], sgn[:, 2:3], 1.0 - SLOPE, vec[:, 7:8], ALU.mult, ALU.mult)\
                .then_inc(s_own, 1)
            dve.wait_ge(s_own, 3)
            V.tensor_scalar(raw[:, 4, :], raw[:, 0, :], sgn[:, 3:4], None, ALU.mult)
            V.tensor_scalar(raw[:, 5, :], raw[:, 1, :], sgn[:, 3:4], None, ALU.mult).then_inc(s_scl, 1)
            V.tensor_scalar(sgn8[:, :], heads[:, :], sgn[:, 2:3], None, ALU.mult).then_inc(s_own, 1)
            dve.wait_ge(s_own, 4)
            dve.wait_ge(s_ones, 2)
            for t in range(4):
                V.tensor_copy(ssum[:, t, t * H:(t + 1) * H], sgn8[:, :])
            for m in range(16):
                V.tensor_scalar(slin[:, m, :], sgn8[:, :], SLOPE / (1.0 - SLOPE), None, ALU.mult)
            for half in range(2):
                for q in range(4):
                    picked = ident[:, :].rearrange("p (c q a t k) -> p c q a t k", c=4, q=4, a=2, k=1)[:, :, q, half]
                    V.tensor_copy(rows[:, half * 4 + q, :, :].rearrange("p (c t) h -> p c t h", c=4),
                                  bcast(picked, [N, 4, 4, H]))
            dve.wait_ge(s_wa, 1)
            V.tensor_copy(wcol[:, :], X1[:, 0:4]).then_inc(s_own, 1)
            dve.wait_ge(s_own, 5)
            V.tensor_copy(w0x[:, F:F + 1], wcol[:, 1:2])
            V.tensor_copy(w1x[:, F:F + 1], wcol[:, 3:4])
            V.tensor_copy(src0[:, :], bcast(wcol[:, 0:1], [F, N]))
            V.tensor_copy(src1[:, :], bcast(wcol[:, 2:3], [F, N]))
            V.tensor_copy(dst1[:, :], bcast(wcol[:, 3:4], [F, N]))
            dve.wait_ge(s_wlr, 1)
            V.tensor_copy(wlT[:, :], X2[:, 0:F])
            V.tensor_copy(wrT[:, :], X2[:, F:2 * F])
            V.tensor_copy(wrnT[:, :], X2[:, 2 * F:3 * F])
            V.tensor_tensor(radial[:, 2:3], radial[:, 0:1], radial[:, 0:1], ALU.mult)
            V.tensor_scalar(radial[:, 4:5], radial[:, 1:2], -1.0, None, ALU.mult).then_inc(s_own, 1)
            dve.wait_ge(s_own, 6)
            V.reciprocal(radial[:, 3:4], radial[:, 2:3])
            V.tensor_scalar(radial[:, 5:6], radial[:, 4:5], 1.0, None, ALU.add).then_inc(s_own, 1)
            dve.wait_ge(s_own, 7)
            V.tensor_tensor(radial[:, 4:6], radial[:, 4:6], radial[:, 4:6], ALU.mult).then_inc(s_own, 1)
            dve.wait_ge(s_own, 8)
            V.tensor_scalar(radial[:, 4:6], radial[:, 4:6], radial[:, 3:4], -0.5, ALU.mult, ALU.mult)\
                .then_inc(s_rade, 1)
            dve.wait_ge(s_hid, 1)
            V.tensor_scalar(filt[:, 0:2], T[:, 0:2], vec[:, 4:5], None, ALU.add).then_inc(s_hidb, 1)
            for k in range(4):
                V.scalar_tensor_tensor(brow[0:1, k, :], T[0:1, F:2 * F], -LOG2, brow[0:1, 4, :], ALU.mult, ALU.add)
            dve.wait_ge(s_soft, 3)
            V.scalar_tensor_tensor(filt[:, 6:8], filt[:, 0:2], 0.0, filt[:, 4:6], ALU.max, ALU.add).then_inc(s_own, 1)
            dve.wait_ge(s_own, 9)
            V.tensor_scalar(filt[:, 6:8], filt[:, 6:8], -LOG2, None, ALU.add).then_inc(s_ssp, 1)
            dve.wait_ge(s_fil, 1)
            V.tensor_scalar(filt[:, 8:9], T[:, 2:3], vec[:, 5:6], CUT0, ALU.add, ALU.mult)
            V.tensor_scalar(filt[:, 10:11], T[:, 3:4], vec[:, 5:6], CUT1, ALU.add, ALU.mult).then_inc(s_own, 1)
            dve.wait_ge(s_own, 10)
            V.tensor_tensor(filt[:, 9:10], filt[:, 10:11], filt[:, 8:9], ALU.subtract).then_inc(s_ready, 1)
            dve.wait_ge(s_ready, 1)

            def tiles(g, step):
                half, t = step // 4, step % 4
                count = DVE_TILES[step]
                wait(dve, s_zu, g.count(STEPS, step + 1 - STEPS))
                minus_gr = ngr[:, g.slot2, :].rearrange("p (i s) -> p i s", s=8)[:, 0:count, step:step + 1]
                V.tensor_tensor(Z[:, half, t, 0:count, :],
                                bcast(GL[g.slot2][:, 0:N].rearrange("p (a j) -> p a j", a=1), [F, count, N]),
                                bcast(minus_gr, [F, count, N]), ALU.max).then_inc(s_zv, 1)

            def moments(g, data, at, s_data, s_stats):
                wait(dve, s_data, g.count(plus=1))
                V.bn_stats(small[:, g.slot2, at:at + 6], data).then_inc(s_stats, 1)

            def variance(g, at, s_var):
                V.bn_aggr(small[:, g.slot2, at + 6:at + 8], small[:, g.slot2, at:at + 6]).then_inc(s_var, 1)

            def period(fours, u):
                a, b, c, d, e = (Item(fours, u - k) for k in range(5))
                on = c.there()
                if on:
                    wait(dve, s_gl, c.count(plus=1))
                    wait(dve, s_ngr, c.count(plus=1))
                    tiles(c, 0)
                if a.there():
                    dve.wait_ge(s_aa[a.slot4], a.loads())
                    wait(dve, s_ck2, a.count(plus=-1))
                    V.scalar_tensor_tensor(chk[:, a.slot2, :], adj_a[:, a.slot4, :], -1.0, adj_a[:, a.slot4, :],
                                           ALU.add, ALU.mult).then_inc(s_ck, 1)
                if on:
                    tiles(c, 1)
                if d.there():
                    wait(dve, s_sc, d.count(2, 2))
                    V.tensor_reduce(negmax[:, d.slot2, 4:8], E[1][:, :].rearrange("p (q j) -> p q j", q=4), X, ALU.max,
                                    negate=True).then_inc(s_mx2, 1)
                if b.there():
                    wait(dve, s_nb1, b.count(plus=1))
                    V.reciprocal(small[:, b.slot2, 21:22], X1[:, 0:1]).then_inc(s_rs1, 1)
                if a.there():
                    wait(dve, s_ck, a.count(plus=1))
                    V.tensor_reduce(chk_all[:, a.columns(1)], chk[:, a.slot2, :], X, ALU.max,
                                    apply_absolute_value=True).then_inc(s_ck2, 1)
                if b.there():
                    wait(dve, s_rs1, b.count(plus=1))
                    V.scalar_tensor_tensor(mix1[:, b.slot2, :], X1[:, 1:F + 1], small[:, b.slot2, 21:22],
                                           nbr1[:, b.slot2, :], ALU.mult, ALU.add).then_inc(s_mix1, 1)
                if b.there():
                    wait(dve, s_mix1, b.count(plus=1))
                    V.scalar_tensor_tensor(act1[:, b.slot2, :], mix1[:, b.slot2, :], SLOPE, mix1[:, b.slot2, :],
                                           ALU.mult, ALU.max).then_inc(s_act1, 1)
                    wait(dve, s_act1, b.count(plus=1))
                    V.tensor_tensor(sum1[:, b.slot2, :], act1[:, b.slot2, :], x1[:, b.slot2, :], ALU.add)\
                        .then_inc(s_sm1, 1)
                    moments(b, sum1[:, b.slot2, :], 32, s_sm1, s_st1)
                    wait(dve, s_st1, b.count(plus=1))
                if on:
                    tiles(c, 2)
                if b.there():
                    variance(b, 32, s_ag1)
                if on:
                    tiles(c, 3)
                if a.there():
                    wait(dve, s_at0, a.count(plus=1))
                    V.reciprocal(small[:, a.slot2, 22:23], X0[:, 0:1]).then_inc(s_rs0, 1)
                    V.tensor_copy(sum_all[:, a.columns(1)], X0[:, 0:1]).then_inc(s_lc, 1)
                if a.there():
                    wait(dve, s_rs0, a.count(plus=1))
                    V.scalar_tensor_tensor(sum0[:, a.slot2, :], X0[:, 1:F + 1], small[:, a.slot2, 22:23],
                                           xin[:, a.slot4, :], ALU.mult, ALU.add).then_inc(s_sm0, 1)
                    moments(a, sum0[:, a.slot2, :], 0, s_sm0, s_st0)
                    wait(dve, s_st0, a.count(plus=1))
                if b.there():
                    wait(dve, s_rd1, b.count(plus=1))
                    V.tensor_scalar(x2[:, b.slot4, :], sum1[:, b.slot2, :], small[:, b.slot2, 38:39],
                                    small[:, b.slot2, 41:42], ALU.subtract, ALU.mult).then_inc(s_x2, 1)
                if a.there():
                    variance(a, 0, s_ag0)
                if on:
                    tiles(c, 4)
                if a.there():
                    wait(dve, s_rd0, a.count(plus=1))
                    V.tensor_scalar(x1[:, a.slot2, :], sum0[:, a.slot2, :], small[:, a.slot2, 6:7],
                                    small[:, a.slot2, 9:10], ALU.subtract, ALU.mult).then_inc(s_x1, 1)
                if on:
                    tiles(c, 5)
                if d.there():
                    wait(dve, s_at2, d.count(plus=1))
                    V.reciprocal(small[:, d.slot2, 24:32],
                                 X2[:, 0:H * HE].rearrange("p (h f) -> p h f", h=H)[:, :, FH]).then_inc(s_rs2, 1)
                    wait(dve, s_rs2, d.count(plus=1))
                    V.tensor_tensor(att2[:, d.slot2, :, :],
                                    X2[:, 0:H * HE].rearrange("p (h f) -> p h f", h=H)[:, :, 0:FH],
                                    bcast(small[:, d.slot2, 24:32].rearrange("p (h k) -> p h k", k=1), [N, H, FH]),
                                    ALU.mult).then_inc(s_nm2, 1)
                    wait(dve, s_nm2, d.count(plus=1))
                    flat = att2[:, d.slot2, :, :].rearrange("p h f -> p (h f)")
                    V.scalar_tensor_tensor(act2[:, d.slot2, :], flat, SLOPE, flat, ALU.mult, ALU.max)\
                        .then_inc(s_act2, 1)
                    wait(dve, s_act2, d.count(plus=1))
                    V.tensor_tensor(sum2[:, d.slot2, :], act2[:, d.slot2, :], x2[:, d.slot4, :], ALU.add)\
                        .then_inc(s_sm2, 1)
                    moments(d, sum2[:, d.slot2, :], 48, s_sm2, s_st2)
                    wait(dve, s_st2, d.count(plus=1))
                if on:
                    wait(dve, s_sc, c.count(2, 1))
                    V.tensor_reduce(negmax[:, c.slot2, 0:4], E[0][:, :].rearrange("p (q j) -> p q j", q=4), X, ALU.max,
                                    negate=True).then_inc(s_mx2, 1)
                if d.there():
                    variance(d, 48, s_ag2)
                if on:
                    tiles(c, 6)
                if a.there():
                    wait(dve, s_p1, a.count(plus=1))
                    V.tensor_reduce(small[:, a.slot2, 20:21], X2[:, 384:512], X, ALU.max).then_inc(s_mx1, 1)
                if d.there():
                    wait(dve, s_rd2, d.count(plus=1))
                    wait(dve, s_x3k[d.slot2], d.loads(2) - 16)
                    V.tensor_scalar(x3[:, d.slot2, :], sum2[:, d.slot2, :], small[:, d.slot2, 54:55],
                                    small[:, d.slot2, 57:58], ALU.subtract, ALU.mult).then_inc(s_x3, 1)
                if on:
                    tiles(c, 7)
                if a.there():
                    wait(dve, s_u1, a.count(plus=1))
                    wait(dve, s_m1, a.count(plus=1))
                    V.tensor_scalar(small[:, a.slot2, 23:24], h1[:, a.slot2, F + 1:F + 2], small[:, a.slot2, 20:21],
                                    SLOPE, ALU.subtract, ALU.mult)
                    V.tensor_tensor(dif1[:, a.slot2, :], relu1[:, a.slot2, :], max1[:, a.slot2, :], ALU.subtract)\
                        .then_inc(s_d1, 1)

            for u in range(RING):
                period(0, u)
            with dve.Fori(1, B // RING) as fours:
                for u in range(RING):
                    period(fours, u)
            for u in range(LAST_STAGE):
                period(B // RING, u)
            last_phase_vector(dve)
            find_verdict(dve)
            where_needed(dve, general_vector)

        @block.gpsimd
        def _(pool):
            G = nc.gpsimd
            G.memset(epses[:, :], EPS)
            G.memset(halves[:, :], -0.5).then_inc(s_cst, 1)
            pool.wait_ge(s_cst, 1)

            def tiles(g, step):
                half, t = step // 4, step % 4
                first = DVE_TILES[step] + ACT_TILES[step]
                wait(pool, s_zu, g.count(STEPS, step + 1 - STEPS))
                minus_gr = ngr[:, g.slot2, :].rearrange("p (i s) -> p i s", s=8)[:, first:TILES, step:step + 1]
                G.tensor_tensor(Z[:, half, t, first:TILES, :], bcast(gl[:, g.slot2:g.slot2 + 1, :], [F, TILES - first, N]),
                                bcast(minus_gr, [F, TILES - first, N]), ALU.subtract).then_inc(s_zp, 1)

            def rstd(g, at, s_var, s_eps, s_rstd):
                wait(pool, s_var, g.count(plus=1))
                G.tensor_tensor(small[:, g.slot2, at + 8:at + 9], small[:, g.slot2, at + 7:at + 8], epses[:, 0:1],
                                ALU.add).then_inc(s_eps, 1)
                wait(pool, s_eps, g.count(plus=1))
                G.tensor_tensor(small[:, g.slot2, at + 9:at + 10], small[:, g.slot2, at + 8:at + 9], halves[:, 0:1],
                                ALU.pow).then_inc(s_rstd, 1)

            def period(fours, u):
                a, b, c, d, e = (Item(fours, u - k) for k in range(5))
                on = c.there()
                if on:
                    wait(pool, s_gl, c.count(plus=1))
                    wait(pool, s_ngr, c.count(plus=1))
                    tiles(c, 0)
                if on:
                    tiles(c, 1)
                if on:
                    tiles(c, 2)
                if c.there():
                    pool.wait_ge(s_ab[c.slot4], c.loads())
                    wait(pool, s_sc, c.count(2, -2))
                if a.there():
                    wait(pool, s_e0, a.count(plus=1))
                    wait(pool, s_at0, a.count(plus=-1))
                    G.tensor_tensor(prob0[:, a.slot2, :], exp0[:, a.slot2, :], xa[:, a.slot2, N:2 * N], ALU.mult)\
                        .then_inc(s_pr0, 1)
                if c.there():
                    G.tensor_scalar(maskb[:, c.slot2, :], adj_b[:, c.slot4, :], MASKED, -MASKED, ALU.mult, ALU.add)\
                        .then_inc(s_mb, 1)
                if b.there():
                    rstd(b, 32, s_ag1, s_ve1, s_rd1)
                if on:
                    tiles(c, 3)
                if a.there():
                    rstd(a, 0, s_ag0, s_ve0, s_rd0)
                if on:
                    tiles(c, 4)
                if on:
                    tiles(c, 5)
                if d.there():
                    rstd(d, 48, s_ag2, s_ve2, s_rd2)
                if on:
                    tiles(c, 6)
                if on:
                    tiles(c, 7)

            for u in range(RING):
                period(0, u)
            with pool.Fori(1, B // RING) as fours:
                for u in range(RING):
                    period(fours, u)
            for u in range(LAST_STAGE):
                period(B // RING, u)
            last_phase_pool(pool)
            where_needed(pool, general_pool)


_INS = ["x", "adj", "L0_gnn_W", "L0_gnn_a", "L1_gnn_W", "L1_gnn_a", "L2_gnn_W_l", "L2_gnn_W_r", "L2_gnn_w_attn",
        "L3_gnn_widths", "L3_gnn_offsets", "L3_gnn_w_in2f", "L3_gnn_fw1", "L3_gnn_fb1", "L3_gnn_fw2", "L3_gnn_fb2",
        "L3_gnn_ow1", "L3_gnn_ob1", "L3_gnn_ow2", "L3_gnn_ob2"]


def kernel(**inputs):
    import numpy as _np
    import concourse.bacc as _bacc
    from concourse import mybir as _mybir
    from concourse.bass_utils import run_bass_kernel_spmd as _run

    nc = _bacc.Bacc("TRN2", target_bir_lowering=False, num_devices=1)
    arrays, args = {}, []
    for name in _INS:
        arrays[name + "_dram"] = _np.ascontiguousarray(inputs[name])
    arrays["ident_dram"] = _np.eye(N, dtype=_np.float32)
    arrays["heads_dram"] = _np.repeat(_np.eye(H, dtype=_np.float32), FH, axis=0)
    for name, a in arrays.items():
        args.append(nc.dram_tensor(name, a.shape, _mybir.dt.from_np(a.dtype), kind="ExternalInput").ap())
    out = nc.dram_tensor("out_dram", (B, N, F), FP32, kind="ExternalOutput").ap()
    build(nc, *args, out)
    r = _run(nc, [arrays], core_ids=[0])
    return r.results[0]["out_dram"]
```

```python
import math
from contextlib import ExitStack

import concourse.bass as bass
from concourse import mybir

FP32 = mybir.dt.float32
BF16 = mybir.dt.bfloat16
I32 = mybir.dt.int32
ALU = mybir.AluOpType
ACT = mybir.ActivationFunctionType
X = mybir.AxisListType.X

B = 64
N = 128
F = 128
H = 8
FH = F // H
R = 20
SLOPE = 0.2
EPS = 1e-5
LOG2 = math.log(2.0)
CUTOFF = 5.0
CUT0 = 1.0
CUT1 = 0.5 * (math.cos(math.pi / CUTOFF) + 1.0)
QUAD = 4
QUADS = B // QUAD
MASKED = 1.0e30
ROUNDER = 1.5 * 2.0 ** 23
RING = 4
STEPS = 8
LAST_STAGE = 4
X3_KEPT = 16 + 16 * B // 2
HE = 2 * FH

TILES = 16
DVE_TILES = [9] * STEPS
ACT_TILES = [1] * STEPS


class Item:

    def __init__(self, turn, offset, body=RING, total=B):
        self.turn, self.offset, self.body, self.total = turn, offset, body, total
        self.static = isinstance(turn, int)
        self.slot4, self.slot2 = offset % 4, offset % 2

    def there(self):
        return not self.static or 0 <= self.body * self.turn + self.offset < self.total

    def count(self, per_item=1, plus=0):
        return (self.body * per_item) * self.turn + (per_item * self.offset + plus)

    def loads(self, slots=RING):
        return (16 * self.body // slots) * self.turn + 16 * (self.offset // slots + 1)

    def columns(self, width=F):
        start = (self.body * width) * self.turn + width * self.offset
        return slice(start, start + width) if self.static else bass.ds(start, width)

    def pick(self, array):
        if self.static:
            return array[self.body * self.turn + self.offset]
        return array[bass.ds(self.body * self.turn + self.offset, 1)].rearrange("a n f -> (a n) f")


class Chain:

    def __init__(self, semaphore, names, turns):
        self.semaphore, self.names, self.turns = semaphore, names.split(), turns

    def after(self, name, outer, turn=0):
        stages = len(self.names)
        index = 0 if name == "start" else self.names.index(name) + 1
        return (stages * self.turns + 1) * outer + stages * turn + (index + 1)


GRAPH_STAGES = """
    turned0 turned0_kept projected0 h0 scores0 edges0 masked0 max0 probs0 probsT0 probsT0_kept attended0 recip0 weight0
    norm0 added0 moments0 seen0 var0 vareps0 rstd0 layer0
    turned1 turned1_kept projected1 h1 scores1 lrelu1 max1 probs1 probsT1 probsT1_kept attended1 recip1 norm1 mixed1
    act1 added1 moments1 seen1 var1 vareps1 rstd1 layer1
    turned2 turned2_kept projected2 projected2_kept pairs
    turned_scores2 weighed2 masked2 max2 shifted2 exps2 edges2 sums2 probsT2 probsT2_kept attended2 recips2 norm2 act2
    added2 moments2 seen2 var2 vareps2 rstd2 layer2
    turned3 turned3_kept projected3 projected3_kept rows hidden3 bias3 abs3 exp3 ln3 softplus3 output3
    added3 moments3 seen3 var3 vareps3 rstd3 layer3
    stored"""
PAIR_STAGES = "added lrelu summed kept"
ROW_STAGES = """
    offset squares exponents rest radial hidden bias abs exp ln softplus ssp filter
    size cosine raised cut weighed messages kept"""


def wait(engine, semaphore, value, most=None):
    if isinstance(value, int):
        if value <= 0:
            return
        if most is not None:
            value = min(value, most)
    engine.wait_ge(semaphore, value)


def build(nc, x, adj, W0, a0, W1, a1, W_l, W_r, w_attn, widths, offsets, w_in2f, fw1, fb1, fw2, fb2,
          ow1, ob1, ow2, ob2, ident_in, heads_in, out):
    ctx = ExitStack()
    with ctx:
        def sb(name, shape, dt=FP32):
            return ctx.enter_context(nc.sbuf_tensor(name, shape, dt))

        def sem(name):
            return ctx.enter_context(nc.semaphore(name))

        ident = sb("ident", [N, N])
        heads = sb("heads", [F, H])
        raw = sb("raw", [F, 8, F])
        vec = sb("vec", [F, 16])
        w0x = sb("w0x", [F, F + 1])
        w1x = sb("w1x", [F, F + 1])
        src0 = sb("src0", [F, N])
        src1 = sb("src1", [F, N])
        dst1 = sb("dst1", [F, N])
        wcol = sb("wcol", [F, 4])
        wlT = sb("wlT", [F, F])
        wrT = sb("wrT", [F, F])
        wrnT = sb("wrnT", [F, F])
        sgn = sb("sgn", [F, 4])
        sgn8 = sb("sgn8", [F, H])
        ssum = sb("ssum", [F, 4, 32])
        slin = sb("slin", [F, 16, H])
        rows = sb("rows", [N, H, 16, H], BF16)
        win = sb("win", [F, F])
        w1f = sb("w1f", [R, F])
        w2f = sb("w2f", [F, F])
        ow1s = sb("ow1s", [F, F])
        ow2s = sb("ow2s", [F, F])
        radial = sb("radial", [R, 8])
        ones = sb("ones", [N, N])
        filt = sb("filt", [F, 12])
        halves = sb("halves", [N, QUAD])
        epses = sb("epses", [N, QUAD])
        brow = sb("brow", [1, 2, F])
        rowb = sb("rowb", [N, F])

        xin = sb("xin", [N, RING, F])
        adj_a = sb("adj_a", [N, RING, N])
        adj_b = sb("adj_b", [N, RING, N])
        xa = sb("xa", [N, 2, 2 * N])
        h0 = sb("h0", [N, 2, F + 2])
        tanh0 = sb("tanh0", [N, 2, N])
        exp0 = sb("exp0", [N, 2, N])
        prob0 = sb("prob0", [N, 2, N])
        chk = sb("chk", [N, 2, N])
        small = sb("small", [N, 2, 64])
        sum0 = sb("sum0", [N, 2, F])
        x1 = sb("x1", [N, 2, F])
        x1T = sb("x1T", [F, 2, N])
        h1 = sb("h1", [N, 2, F + 2])
        relu1 = sb("relu1", [N, 2, N])
        max1 = sb("max1", [N, 2, N])
        dif1 = sb("dif1", [N, 2, N])
        prob1 = sb("prob1", [N, 2, N])
        nbr1 = sb("nbr1", [N, 2, F])
        mix1 = sb("mix1", [N, 2, F])
        act1 = sb("act1", [N, 2, F])
        sum1 = sb("sum1", [N, 2, F])
        x2 = sb("x2", [N, RING, F])
        x2T = sb("x2T", [F, 2, N])
        gl = sb("gl", [F, 2, N])
        gr = sb("gr", [F, 2, N])
        ngr = sb("ngr", [F, 2, N])
        grx = sb("grx", [N, 2, H, HE])
        Z = sb("Z", [F, 2, 4, TILES, N])
        maskb = sb("maskb", [N, 2, N], BF16)
        negmax = sb("negmax", [N, 2, 8])
        prob2 = sb("prob2", [N, 2, 4, N])
        pT = sb("pT", [N, 4, 4, 2, 32])
        sT2 = sb("sT2", [N, 2, 2 * N])
        att2 = sb("att2", [N, 2, H, FH])
        act2 = sb("act2", [N, 2, F])
        sum2 = sb("sum2", [N, 2, F])
        x3 = sb("x3", [N, 2, F])
        xa3 = sb("xa3", [N, 2, 2 * N + 1])
        y3 = sb("y3", [N, 2, F])
        ysum = sb("ysum", [F, 2, 1])
        x3_all = sb("x3_all", [N, B * F])
        agg_all = sb("agg_all", [F, B * N])
        chk_all = sb("chk_all", [N, B])
        sum_all = sb("sum_all", [N, B])
        deg_all = sb("deg_all", [N, B])
        verdict = sb("verdict", [N, 8])
        flag = sb("flag", [1, 1], I32)

        bank = [ctx.enter_context(nc.psum_tensor(f"bank{i}", [128, 512], FP32)) for i in range(8)]
        X0, X1, X2, T = bank[0], bank[1], bank[2], bank[3]
        GL = bank[4:6]
        E = bank[6:8]

        s_w = sem("weights_loaded")
        s_ones = sem("ones_set")
        s_own = sem("vector_own_order")
        s_wT = sem("w0_w1_transposed")
        s_wTC = sem("w0_w1_transposed_copied")
        s_wa = sem("w_times_a")
        s_scl = sem("w_l_w_r_scaled")
        s_wlr = sem("w_l_w_r_transposed")
        s_rade = sem("radial_exponents")
        s_rad = sem("radial_values")
        s_hid = sem("filter_hidden")
        s_row = sem("output_row")
        s_hidb = sem("filter_hidden_bias")
        s_soft = sem("filter_softplus")
        s_ssp = sem("filter_ssp")
        s_fil = sem("filter_values")
        s_ready = sem("constants_ready")
        s_x = [sem(f"x_loaded{i}") for i in range(RING)]
        s_aa = [sem(f"adj_a_loaded{i}") for i in range(RING)]
        s_ab = [sem(f"adj_b_loaded{i}") for i in range(RING)]
        s_xaT = sem("x_adj_transposed")
        s_xaC = sem("x_adj_copied")
        s_p0 = sem("projected0")
        s_h0 = sem("h0_copied")
        s_th = sem("tanh_done")
        s_e0 = sem("exp0_done")
        s_pr0 = sem("prob0_done")
        s_at0 = sem("attended0")
        s_rs0 = sem("recip0")
        s_sm0 = sem("sum0_done")
        s_st0 = sem("stats0")
        s_ag0 = sem("var0")
        s_ve0 = sem("var0_eps")
        s_rd0 = sem("rstd0")
        s_x1 = sem("x1_done")
        s_ck = sem("chk_done")
        s_lc = sem("sum_kept")
        s_x1T = sem("x1_transposed")
        s_x1C = sem("x1T_copied")
        s_p1 = sem("projected1")
        s_mx1 = sem("smax_done")
        s_h1 = sem("h1_copied")
        s_u1 = sem("relu1_done")
        s_m1 = sem("max1_done")
        s_d1 = sem("dif1_done")
        s_dt1 = sem("target_dif1_done")
        s_e1 = sem("prob1_done")
        s_at1 = sem("attended1")
        s_nb1 = sem("nbr1_copied")
        s_rs1 = sem("recip1")
        s_mix1 = sem("mix1_done")
        s_act1 = sem("act1_done")
        s_sm1 = sem("sum1_done")
        s_st1 = sem("stats1")
        s_ag1 = sem("var1")
        s_ve1 = sem("var1_eps")
        s_rd1 = sem("rstd1")
        s_x2 = sem("x2_done")
        s_x2T = sem("x2_transposed")
        s_x2C = sem("x2T_copied")
        s_p2 = sem("projected2")
        s_gl = sem("gl_copied")
        s_gr = sem("gr_copied")
        s_ngr = sem("ngr_copied")
        s_grx = sem("grx_copied")
        s_mb = sem("mask_bias")
        s_zv = sem("tiles_vector")
        s_za = sem("tiles_scalar")
        s_zp = sem("tiles_pool")
        s_zu = sem("tiles_summed")
        s_sc = sem("scores_done")
        s_mx2 = sem("max2_done")
        s_e2 = sem("prob2_done")
        s_pT = sem("prob2_transposed")
        s_pC = sem("pT_copied")
        s_sT2 = sem("attended2_by_feature")
        s_sT2C = sem("attended2_by_feature_copied")
        s_at2 = sem("attended2")
        s_rs2 = sem("recip2")
        s_nm2 = sem("att2_done")
        s_act2 = sem("act2_done")
        s_sm2 = sem("sum2_done")
        s_st2 = sem("stats2")
        s_ag2 = sem("var2")
        s_ve2 = sem("var2_eps")
        s_rd2 = sem("rstd2")
        s_x3 = sem("x3_done")
        s_x3k = [sem(f"x3_kept{i}") for i in range(2)]
        s_x3T = sem("x3_adj_transposed")
        s_x3C = sem("x3_adj_copied")
        s_y3 = sem("y3_projected")
        s_y3C = sem("y3_copied")
        s_ag3 = sem("aggregated3")
        s_ys = sem("ysum_done")
        s_agC = sem("agg_kept")

        s_cst = sem("minus_half_set")
        s_bz = sem("out_hidden")
        s_ba = sem("out_abs")
        s_be = sem("out_exp")
        s_bl = sem("out_log")
        s_bmx = sem("out_ssp")
        s_bo = sem("out_projected")
        s_xr = sem("out_row_added")
        s_br = sem("out_residual")
        s_bs = sem("out_stats")
        s_bv = sem("out_var")
        s_bve = sem("out_var_eps")
        s_brd = sem("out_rstd")
        s_bnb = sem("out_shift")
        s_by = sem("out_normed")
        s_store = [sem(f"stored{i}") for i in range(4)]

        space = Z[:, :, :, :, :].rearrange("p a b c j -> p (a b c j)")

        def last(k):
            return space[:, k * 4 * QUAD * N:(k + 1) * 4 * QUAD * N].rearrange("p (a n) -> p a n", a=4)

        absz, expz, lnz, ssp, res, fin = (last(k) for k in range(6))
        mom = sb("mom", [N, 4, QUAD, 16])

        block = ctx.enter_context(nc.Block())

        def bcast(ap, shape):
            return ap.to_broadcast(shape)


        hidden = [X0, X1, GL[0], GL[1]]
        outs = [X2, T, E[0], E[1]]

        def in_last_phase(engine, period):
            for turn in range(2):
                for u in range(4):
                    period(turn, u)
            with engine.Fori(2, QUADS // 4) as turn:
                for u in range(4):
                    period(turn, u)
            for u in range(5):
                period(QUADS // 4, u)

        def fours_of(turn, u):
            return (Item(turn, u - k, 4, QUADS) for k in range(6))

        def last_phase_sync(sp):
            def period(turn, u):
                a, b, c, d, e, f = fours_of(turn, u)
                if f.there():
                    source = fin[:, f.slot4, :].rearrange("p (g f) -> p g f", g=QUAD)
                    if f.static:
                        first = QUAD * (4 * f.turn + f.offset)
                        to = out[first:first + QUAD]
                    else:
                        to = out[bass.ds(QUAD * 4 * f.turn + QUAD * f.offset, QUAD)]
                    wait(sp, s_by, f.count(plus=1))
                    sp.dma_start(to.rearrange("g n f -> n g f"), source).then_inc(s_store[f.slot4], 16)

            in_last_phase(sp, period)
            for k in range(4):
                sp.wait_ge(s_store[k], 16 + 16 * QUADS // 4)

        def last_phase_tensor(pe):
            mm = nc.tensor.matmul
            pe.wait_ge(s_agC, B)
            pe.wait_ge(s_e2, 2 * B)

            def period(turn, u):
                a, b, c, d, e, f = fours_of(turn, u)
                if a.there():
                    mm(hidden[a.slot4][:, :], ow1s[:, :], agg_all[:, a.columns(QUAD * N)], start=True, stop=True)\
                        .then_inc(s_bz, 1)
                if c.there():
                    wait(pe, s_bmx, c.count(plus=1))
                    for g in range(QUAD):
                        ins = mm(outs[c.slot4][:, g * F:(g + 1) * F], ssp[:, c.slot4, g * N:(g + 1) * N], ow2s[:, :],
                                 start=True, stop=True)
                    ins.then_inc(s_bo, 1)

            in_last_phase(pe, period)

        def last_phase_scalar(act):
            A = nc.scalar.activation
            nc.scalar.preload_act_table_set("natural_log_exp_and_others")

            def period(turn, u):
                a, b, c, d, e, f = fours_of(turn, u)

                def normed(groups):
                    for g in groups:
                        ins = A(fin[:, f.slot4, g * F:(g + 1) * F], res[:, f.slot4, g * F:(g + 1) * F], ACT.Identity,
                                scale=mom[:, f.slot4, g, 9:10], bias=mom[:, f.slot4, g, 10:11])
                    return ins

                if b.there():
                    wait(act, s_bz, b.count(plus=1))
                    wait(act, s_zu, B * STEPS)
                    A(absz[:, b.slot4, :], hidden[b.slot4][:, :], ACT.Abs, bias=vec[:, 6:7]).then_inc(s_ba, 1)
                if f.there():
                    wait(act, s_bnb, f.count(plus=1))
                    wait(act, s_store[f.slot4], f.loads(4))
                    normed((0,))
                if b.there():
                    wait(act, s_ba, b.count(plus=1))
                    A(expz[:, b.slot4, :], absz[:, b.slot4, :], ACT.Exp, scale=-1.0).then_inc(s_be, 1)
                if f.there():
                    normed((1,))
                if b.there():
                    wait(act, s_be, b.count(plus=1))
                    A(lnz[:, b.slot4, :], expz[:, b.slot4, :], ACT.Ln, bias=1.0).then_inc(s_bl, 1)
                if f.there():
                    normed((2, 3)).then_inc(s_by, 1)

            in_last_phase(act, period)

        def last_phase_vector(dve):
            V = nc.vector
            dve.wait_ge(s_x3k[0], X3_KEPT)
            dve.wait_ge(s_x3k[1], X3_KEPT)

            def period(turn, u):
                a, b, c, d, e, f = fours_of(turn, u)
                if c.there():
                    wait(dve, s_bl, c.count(plus=1))
                    V.scalar_tensor_tensor(ssp[:, c.slot4, :], hidden[c.slot4][:, :], vec[:, 8:9], lnz[:, c.slot4, :],
                                           ALU.max, ALU.add).then_inc(s_bmx, 1)
                if d.there():
                    wait(dve, s_bo, d.count(plus=1))
                    wait(dve, s_xr, d.count(plus=1))
                    wait(dve, s_by, d.count(plus=-3))
                    V.tensor_tensor(res[:, d.slot4, :], outs[d.slot4][:, :], x3_all[:, d.columns(QUAD * F)],
                                    ALU.add).then_inc(s_br, 1)
                    wait(dve, s_br, d.count(plus=1))
                    for g in range(QUAD):
                        ins = V.bn_stats(mom[:, d.slot4, g, 0:6], res[:, d.slot4, g * F:(g + 1) * F])
                    ins.then_inc(s_bs, 1)
                    wait(dve, s_bs, d.count(plus=1))
                if e.there():
                    wait(dve, s_brd, e.count(plus=1))
                    V.scalar_tensor_tensor(mom[:, e.slot4, :, 10], mom[:, e.slot4, :, 6], -1.0,
                                           mom[:, e.slot4, :, 9], ALU.mult, ALU.mult).then_inc(s_bnb, 1)
                if d.there():
                    for g in range(QUAD):
                        ins = V.bn_aggr(mom[:, d.slot4, g, 6:8], mom[:, d.slot4, g, 0:6])
                    ins.then_inc(s_bv, 1)

            in_last_phase(dve, period)

        def last_phase_pool(pool):
            G = nc.gpsimd
            pool.wait_ge(s_x3k[0], X3_KEPT)
            pool.wait_ge(s_x3k[1], X3_KEPT)

            def period(turn, u):
                a, b, c, d, e, f = fours_of(turn, u)
                if b.there():
                    kept = x3_all[:, b.columns(QUAD * F)].rearrange("p (g f) -> p g f", g=QUAD)
                    G.tensor_tensor(kept, kept, bcast(rowb[:, :].rearrange("p (k f) -> p k f", k=1), [N, QUAD, F]),
                                    ALU.add).then_inc(s_xr, 1)
                if d.there():
                    wait(pool, s_bv, d.count(plus=1))
                    G.tensor_tensor(mom[:, d.slot4, :, 8], mom[:, d.slot4, :, 7], epses[:, :], ALU.add)\
                        .then_inc(s_bve, 1)
                    wait(pool, s_bve, d.count(plus=1))
                    G.tensor_tensor(mom[:, d.slot4, :, 9], mom[:, d.slot4, :, 8], halves[:, :], ALU.pow)\
                        .then_inc(s_brd, 1)

            in_last_phase(pool, period)


        s_verdict = sem("verdict_parts")
        s_vsum = sem("verdict_summed")
        s_flag = sem("flag_ready")
        s_gx = sem("general_x_loaded")
        s_ga = sem("general_adj_loaded")
        s_gd = sem("general_rows_loaded")
        s_gout = sem("general_out_stored")
        graph = Chain(sem("general_graph_stages"), GRAPH_STAGES, 1)
        pairs = Chain(sem("general_pair_stages"), PAIR_STAGES, N // 4)
        rows3 = Chain(sem("general_row_stages"), ROW_STAGES, N // 4)

        used = [0]

        def room(cols):
            used[0] += cols
            assert used[0] <= 2 * 4 * TILES * N
            return space[:, used[0] - cols:used[0]]

        g_x = [room(F) for _ in range(5)]
        g_adj, g_adjT, g_xT, g_dst0 = (room(N) for _ in range(4))
        g_h = room(F + 1)
        g_score, g_edge, g_masked, g_prob, g_probT = (room(N) for _ in range(5))
        g_norm, g_mix, g_act, g_sum = (room(F) for _ in range(4))
        g_small = room(64)
        g_gl, g_gr, g_grn = (room(N) for _ in range(3))
        g_pair, g_pairL = room(4 * N), room(4 * N)
        g_e, g_e2 = room(H * N), room(H * N)
        g_none = room(N)
        g_sgn = room(H)
        g_d, g_dif, g_rad, g_z, g_y, g_w = (room(4 * N) for _ in range(6))
        g_turn, g_whole, g_cut = (room(4 * N) for _ in range(3))
        g_yT, g_agg = room(N), room(N)
        g_bias = room(1)

        def four(ap):
            return ap.rearrange("p (q j) -> p q j", j=N)

        def general_sync(sp):
            every_row = adj.rearrange("g i j -> (g i) j")
            with sp.Fori(0, B) as g:
                sp.dma_start(g_x[0], x[bass.ds(g, 1)].rearrange("a n f -> (a n) f")).then_inc(s_gx, 16)
                sp.dma_start(g_adj, adj[bass.ds(g, 1)].rearrange("a n f -> (a n) f")).then_inc(s_ga, 16)
                with sp.Fori(0, N // 4) as i:
                    four_rows = every_row[bass.ds(N * g + 4 * i, 4)].rearrange("(a q) j -> a q j", a=1)
                    sp.wait_ge(rows3.semaphore, rows3.after("start", g, i))
                    sp.dma_start(four(g_d), four_rows.to_broadcast([N, 4, N])).then_inc(s_gd, 16)
                sp.wait_ge(graph.semaphore, graph.after("layer3", g))
                sp.dma_start(out[bass.ds(g, 1)].rearrange("a n f -> (a n) f"), g_x[4]).then_inc(s_gout, 16)
                sp.wait_ge(s_gout, 16 * g + 16)
                sp.sem_inc(graph.semaphore, 1)

        def general_tensor(pe):
            mm = nc.tensor.matmul
            turn = nc.tensor.transpose
            done = graph.semaphore
            with pe.Fori(0, B) as g:
                pe.wait_ge(s_gx, 16 * g + 16)
                pe.wait_ge(s_ga, 16 * g + 16)
                pe.wait_ge(done, graph.after("start", g))
                for layer, weight in ((0, w0x), (1, w1x)):
                    if layer:
                        pe.wait_ge(done, graph.after("layer0", g))
                    turn(X1[:, 0:N], g_adj, ident[:, :])
                    turn(X0[:, 0:N], g_x[layer], ident[:, :]).then_inc(done, 1)
                    pe.wait_ge(done, graph.after(f"turned{layer}_kept", g))
                    mm(X0[:, 0:F], g_xT, weight[:, 0:F], start=True, stop=True)
                    mm(X0[:, F:F + 1], g_xT, wcol[:, 2 * layer:2 * layer + 1], start=True, stop=True)
                    mm(X0[:, 2 * F:2 * F + N], (g_dst0, dst1[:, :])[layer], g_xT, start=True, stop=True)\
                        .then_inc(done, 1)
                    pe.wait_ge(done, graph.after(f"probs{layer}", g))
                    turn(X2[:, 0:N], g_prob, ident[:, :]).then_inc(done, 1)
                    pe.wait_ge(done, graph.after(f"probsT{layer}_kept", g))
                    mm(X0[:, 0:F], g_probT, g_h[:, 0:F], start=True, stop=True)
                    mm(X0[:, F:2 * F], g_adjT, g_h[:, 0:F], start=True, stop=True).then_inc(done, 1)
                pe.wait_ge(done, graph.after("layer1", g))
                turn(X0[:, 0:N], g_x[2], ident[:, :]).then_inc(done, 1)
                pe.wait_ge(done, graph.after("turned2_kept", g))
                mm(X0[:, 0:N], wlT[:, :], g_xT, start=True, stop=True)
                mm(X0[:, N:2 * N], wrT[:, :], g_xT, start=True, stop=True)
                mm(X0[:, 2 * N:3 * N], g_xT, wrnT[:, :], start=True, stop=True).then_inc(done, 1)
                with pe.Fori(0, N // 4) as i:
                    pe.wait_ge(pairs.semaphore, pairs.after("lrelu", g, i))
                    for k in range(4):
                        ins = mm(X1[:, k * H:(k + 1) * H], g_pairL[:, k * N:(k + 1) * N], g_sgn,
                                 start=True, stop=True)
                    ins.then_inc(pairs.semaphore, 1)
                pe.wait_ge(done, graph.after("pairs", g))
                for h in range(H):
                    ins = turn((X0, X1)[h // 4][:, h % 4 * N:(h % 4 + 1) * N],
                               g_e.rearrange("p (i h) -> p i h", h=H)[:, :, h], ident[:, :])
                ins.then_inc(done, 1)
                pe.wait_ge(done, graph.after("sums2", g))
                for h in range(H):
                    ins = turn((X0, X1)[h // 4][:, h % 4 * N:(h % 4 + 1) * N], g_e2[:, h * N:(h + 1) * N],
                               ident[:, :])
                ins.then_inc(done, 1)
                pe.wait_ge(done, graph.after("probsT2_kept", g))
                for h in range(H):
                    ins = mm(X2[:, h * FH:(h + 1) * FH], g_e[:, h * N:(h + 1) * N], g_grn[:, h * FH:(h + 1) * FH],
                             start=True, stop=True)
                ins.then_inc(done, 1)
                pe.wait_ge(done, graph.after("layer2", g))
                turn(X0[:, 0:N], g_x[3], ident[:, :]).then_inc(done, 1)
                pe.wait_ge(done, graph.after("turned3_kept", g))
                mm(X0[:, 0:N], win[:, :], g_xT, start=True, stop=True).then_inc(done, 1)
                with pe.Fori(0, N // 4) as i:
                    pe.wait_ge(rows3.semaphore, rows3.after("radial", g, i))
                    mm(X1[:, :], w1f[:, :], g_rad[0:R, :], start=True, stop=True).then_inc(rows3.semaphore, 1)
                    pe.wait_ge(rows3.semaphore, rows3.after("ssp", g, i))
                    mm(X2[:, :], w2f[:, :], g_w, start=True, stop=True).then_inc(rows3.semaphore, 1)
                pe.wait_ge(done, graph.after("rows", g))
                mm(X0[:, 0:N], ow1s[:, :], g_agg, start=True, stop=True).then_inc(done, 1)
                pe.wait_ge(done, graph.after("softplus3", g))
                mm(X2[:, 0:F], ones[0:1, :], brow[0:1, 0, :], start=True, stop=False)
                mm(X2[:, 0:F], g_act, ow2s[:, :], start=False, stop=True).then_inc(done, 1)

        def general_scalar(act):
            A = nc.scalar.activation
            done = graph.semaphore
            with act.Fori(0, B) as g:
                for layer in range(2):
                    act.wait_ge(done, graph.after(f"turned{layer}", g))
                    A(g_adjT, X1[:, 0:N], ACT.Copy)
                    A(g_xT, X0[:, 0:N], ACT.Copy).then_inc(done, 1)
                    act.wait_ge(done, graph.after(f"h{layer}", g))
                    A(g_score, X0[:, 2 * F:2 * F + N], (ACT.Tanh, ACT.Identity)[layer], bias=g_h[:, F:F + 1])\
                        .then_inc(done, 1)
                    act.wait_ge(done, graph.after(f"max{layer}", g))
                    A(g_prob, g_masked, ACT.Exp, bias=g_small[:, 0:1], accum_out=g_small[:, 1:2]).then_inc(done, 1)
                    act.wait_ge(done, graph.after(f"probsT{layer}", g))
                    A(g_probT, X2[:, 0:N], ACT.Copy).then_inc(done, 1)
                act.wait_ge(done, graph.after("turned2", g))
                A(g_xT, X0[:, 0:N], ACT.Copy).then_inc(done, 1)
                act.wait_ge(done, graph.after("projected2", g))
                A(g_gl, X0[:, 0:N], ACT.Copy)
                A(g_gr, X0[:, N:2 * N], ACT.Copy)
                A(g_grn, X0[:, 2 * N:3 * N], ACT.Copy).then_inc(done, 1)
                with act.Fori(0, N // 4) as i:
                    act.wait_ge(pairs.semaphore, pairs.after("summed", g, i))
                    A(g_e[:, bass.ds(4 * H * i, 4 * H)], X1[:, 0:4 * H], ACT.Copy).then_inc(pairs.semaphore, 1)
                act.wait_ge(done, graph.after("shifted2", g))
                A(g_e, g_e2, ACT.Exp).then_inc(done, 1)
                act.wait_ge(done, graph.after("probsT2", g))
                A(g_e[:, 0:4 * N], X0[:, :], ACT.Copy)
                A(g_e[:, 4 * N:8 * N], X1[:, :], ACT.Copy).then_inc(done, 1)
                act.wait_ge(done, graph.after("turned3", g))
                A(g_xT, X0[:, 0:N], ACT.Copy).then_inc(done, 1)
                act.wait_ge(done, graph.after("projected3", g))
                A(g_yT, X0[:, 0:N], ACT.Copy).then_inc(done, 1)
                with act.Fori(0, N // 4) as i:
                    act.wait_ge(rows3.semaphore, rows3.after("rest", g, i))
                    A(g_rad[0:R, :], g_dif[0:R, :], ACT.Exp).then_inc(rows3.semaphore, 1)
                    act.wait_ge(rows3.semaphore, rows3.after("bias", g, i))
                    A(g_y, g_z, ACT.Abs).then_inc(rows3.semaphore, 1)
                    act.wait_ge(rows3.semaphore, rows3.after("abs", g, i))
                    A(g_y, g_y, ACT.Exp, scale=-1.0).then_inc(rows3.semaphore, 1)
                    act.wait_ge(rows3.semaphore, rows3.after("exp", g, i))
                    A(g_y, g_y, ACT.Ln, bias=1.0).then_inc(rows3.semaphore, 1)
                    act.wait_ge(rows3.semaphore, rows3.after("filter", g, i))
                    A(g_turn, g_turn, ACT.Abs).then_inc(rows3.semaphore, 1)
                    act.wait_ge(rows3.semaphore, rows3.after("size", g, i))
                    A(g_turn, g_turn, ACT.Sin, scale=-2.0 * math.pi, bias=g_bias[:, 0:1]).then_inc(rows3.semaphore, 1)
                act.wait_ge(done, graph.after("bias3", g))
                A(g_mix, g_norm, ACT.Abs).then_inc(done, 1)
                act.wait_ge(done, graph.after("abs3", g))
                A(g_mix, g_mix, ACT.Exp, scale=-1.0).then_inc(done, 1)
                act.wait_ge(done, graph.after("exp3", g))
                A(g_mix, g_mix, ACT.Ln, bias=1.0).then_inc(done, 1)

        def general_pool(pool):
            G = nc.gpsimd
            done = graph.semaphore
            with pool.Fori(0, B) as g:
                for layer in range(4):
                    pool.wait_ge(done, graph.after(f"var{layer}", g))
                    G.tensor_tensor(g_small[:, 10:11], g_small[:, 9:10], epses[:, 0:1], ALU.add).then_inc(done, 1)
                    pool.wait_ge(done, graph.after(f"vareps{layer}", g))
                    G.tensor_tensor(g_small[:, 11:12], g_small[:, 10:11], halves[:, 0:1], ALU.pow).then_inc(done, 1)

        def general_vector(dve):
            V = nc.vector
            done = graph.semaphore

            def normalize(g, layer):
                dve.wait_ge(done, graph.after(f"added{layer}", g))
                V.bn_stats(g_small[:, 2:8], g_sum).then_inc(done, 1)
                dve.wait_ge(done, graph.after(f"moments{layer}", g))
                dve.sem_inc(done, 1)
                V.bn_aggr(g_small[:, 8:10], g_small[:, 2:8]).then_inc(done, 1)
                dve.wait_ge(done, graph.after(f"rstd{layer}", g))
                V.tensor_scalar(g_x[layer + 1], g_sum, g_small[:, 8:9], g_small[:, 11:12],
                                ALU.subtract, ALU.mult).then_inc(done, 1)

            dve.wait_ge(s_gx, 16)
            V.memset(g_bias[:, 0:1], math.pi / 2)
            V.tensor_copy(g_dst0, bcast(wcol[:, 1:2], [F, N]))
            V.tensor_scalar(g_sgn, sgn8[:, :], 1.0 / (1.0 - SLOPE), None, ALU.mult).then_inc(s_own, 1)
            dve.wait_ge(s_own, 11)
            with dve.Fori(0, B) as g:
                dve.wait_ge(s_gx, 16 * g + 16)
                dve.wait_ge(s_ga, 16 * g + 16)
                V.tensor_scalar(g_edge, g_adj, 0.0, None, ALU.is_gt)
                V.tensor_scalar(g_none, g_adj, 0.0, None, ALU.is_equal).then_inc(done, 1)
                for layer in range(2):
                    dve.wait_ge(done, graph.after(f"projected{layer}", g))
                    V.tensor_copy(g_h, X0[:, 0:F + 1]).then_inc(done, 1)
                    dve.wait_ge(done, graph.after(f"scores{layer}", g))
                    if layer == 0:
                        V.tensor_tensor(g_prob, g_score, g_edge, ALU.mult)
                        V.tensor_scalar(g_mix, g_edge, 1.0e15, -1.0e15, ALU.mult, ALU.add).then_inc(done, 1)
                        dve.wait_ge(done, graph.after("edges0", g))
                        V.tensor_tensor(g_masked, g_prob, g_mix, ALU.add).then_inc(done, 1)
                        dve.wait_ge(done, graph.after("masked0", g))
                    else:
                        V.scalar_tensor_tensor(g_masked, g_score, SLOPE, g_score, ALU.mult, ALU.max)\
                            .then_inc(done, 1)
                        dve.wait_ge(done, graph.after("lrelu1", g))
                    V.tensor_reduce(g_small[:, 0:1], g_masked, X, ALU.max, negate=True).then_inc(done, 1)
                    dve.wait_ge(done, graph.after(f"attended{layer}", g))
                    V.tensor_reduce(g_small[:, 13:14], g_adjT, X, ALU.add)
                    V.reciprocal(g_small[:, 12:13], g_small[:, 1:2]).then_inc(done, 1)
                    dve.wait_ge(done, graph.after(f"recip{layer}", g))
                    if layer == 0:
                        V.tensor_scalar(g_small[:, 14:15], g_small[:, 13:14], 0.0, 1.0, ALU.is_equal, ALU.add)
                        V.tensor_scalar(g_small[:, 15:16], g_small[:, 13:14], 0.0, g_small[:, 12:13],
                                        ALU.not_equal, ALU.mult).then_inc(done, 1)
                        dve.wait_ge(done, graph.after("weight0", g))
                        V.tensor_scalar(g_norm, X0[:, 0:F], g_small[:, 15:16], None, ALU.mult).then_inc(done, 1)
                        dve.wait_ge(done, graph.after("norm0", g))
                        V.scalar_tensor_tensor(g_sum, g_x[0], g_small[:, 14:15], g_norm, ALU.mult, ALU.add)\
                            .then_inc(done, 1)
                    else:
                        V.tensor_scalar(g_norm, X0[:, 0:F], g_small[:, 12:13], None, ALU.mult).then_inc(done, 1)
                        dve.wait_ge(done, graph.after("norm1", g))
                        V.tensor_tensor(g_mix, g_norm, X0[:, F:2 * F], ALU.add).then_inc(done, 1)
                        dve.wait_ge(done, graph.after("mixed1", g))
                        V.scalar_tensor_tensor(g_act, g_mix, SLOPE, g_mix, ALU.mult, ALU.max).then_inc(done, 1)
                        dve.wait_ge(done, graph.after("act1", g))
                        V.tensor_tensor(g_sum, g_act, g_x[1], ALU.add).then_inc(done, 1)
                    normalize(g, layer)
                dve.wait_ge(done, graph.after("projected2_kept", g))
                dve.sem_inc(pairs.semaphore, 1)
                with dve.Fori(0, N // 4) as i:
                    dve.wait_ge(pairs.semaphore, pairs.after("start", g, i))
                    V.tensor_tensor(four(g_pair), bcast(g_gl.rearrange("p (a j) -> p a j", a=1), [F, 4, N]),
                                    bcast(g_gr[:, bass.ds(4 * i, 4)].rearrange("p (a k) -> p a k", k=1), [F, 4, N]),
                                    ALU.add).then_inc(pairs.semaphore, 1)
                    dve.wait_ge(pairs.semaphore, pairs.after("added", g, i))
                    V.scalar_tensor_tensor(g_pairL, g_pair, SLOPE, g_pair, ALU.mult, ALU.max)\
                        .then_inc(pairs.semaphore, 1)
                dve.wait_ge(pairs.semaphore, pairs.after("kept", g, N // 4 - 1))
                dve.sem_inc(done, 1)
                dve.wait_ge(done, graph.after("turned_scores2", g))
                for k in range(2):
                    V.tensor_tensor(four(g_e2[:, k * 4 * N:(k + 1) * 4 * N]), four((X0, X1)[k][:, :]),
                                    bcast(g_adj.rearrange("p (a j) -> p a j", a=1), [N, 4, N]), ALU.mult)
                V.tensor_scalar(g_mix, g_none, -MASKED, None, ALU.mult).then_inc(done, 1)
                dve.wait_ge(done, graph.after("weighed2", g))
                V.tensor_tensor(four(g_e), four(g_e2), bcast(g_mix.rearrange("p (a j) -> p a j", a=1), [N, H, N]),
                                ALU.add).then_inc(done, 1)
                dve.wait_ge(done, graph.after("masked2", g))
                V.tensor_scalar(g_mix, g_none, -1.0, 1.0, ALU.mult, ALU.add)
                V.tensor_reduce(g_small[:, 16:16 + H], four(g_e), X, ALU.max, negate=True).then_inc(done, 1)
                dve.wait_ge(done, graph.after("max2", g))
                V.tensor_tensor(four(g_e2), four(g_e),
                                bcast(g_small[:, 16:16 + H].rearrange("p (h k) -> p h k", k=1), [N, H, N]),
                                ALU.add).then_inc(done, 1)
                dve.wait_ge(done, graph.after("exps2", g))
                V.tensor_tensor(four(g_e2), four(g_e), bcast(g_mix.rearrange("p (a j) -> p a j", a=1), [N, H, N]),
                                ALU.mult).then_inc(done, 1)
                dve.wait_ge(done, graph.after("edges2", g))
                V.tensor_reduce(g_small[:, 24:24 + H], four(g_e2), X, ALU.add).then_inc(done, 1)
                dve.wait_ge(done, graph.after("attended2", g))
                V.reciprocal(g_small[:, 32:32 + H], g_small[:, 24:24 + H]).then_inc(done, 1)
                dve.wait_ge(done, graph.after("recips2", g))
                V.tensor_tensor(g_norm.rearrange("p (h f) -> p h f", h=H),
                                X2[:, 0:F].rearrange("p (h f) -> p h f", h=H),
                                bcast(g_small[:, 32:32 + H].rearrange("p (h k) -> p h k", k=1), [N, H, FH]),
                                ALU.mult).then_inc(done, 1)
                dve.wait_ge(done, graph.after("norm2", g))
                V.scalar_tensor_tensor(g_act, g_norm, SLOPE, g_norm, ALU.mult, ALU.max).then_inc(done, 1)
                dve.wait_ge(done, graph.after("act2", g))
                V.tensor_tensor(g_sum, g_act, g_x[2], ALU.add).then_inc(done, 1)
                normalize(g, 2)
                dve.wait_ge(done, graph.after("projected3_kept", g))
                dve.sem_inc(rows3.semaphore, 1)
                with dve.Fori(0, N // 4) as i:
                    step = rows3.semaphore
                    dve.wait_ge(s_gd, (16 * N // 4) * g + 16 * i + 16)
                    dve.wait_ge(step, rows3.after("start", g, i))
                    V.tensor_scalar(g_dif[0:R, :], g_d[0:R, :], radial[:, 1:2], None, ALU.subtract)
                    V.tensor_scalar(g_turn, g_d, 0.5 / CUTOFF, None, ALU.mult)
                    V.tensor_scalar(g_cut, g_d, CUTOFF, None, ALU.is_lt).then_inc(step, 1)
                    dve.wait_ge(step, rows3.after("offset", g, i))
                    V.tensor_tensor(g_dif[0:R, :], g_dif[0:R, :], g_dif[0:R, :], ALU.mult)
                    V.tensor_scalar(g_whole, g_turn, ROUNDER, None, ALU.add).then_inc(step, 1)
                    dve.wait_ge(step, rows3.after("squares", g, i))
                    V.tensor_scalar(g_dif[0:R, :], g_dif[0:R, :], radial[:, 3:4], -0.5, ALU.mult, ALU.mult)
                    V.tensor_scalar(g_whole, g_whole, -ROUNDER, None, ALU.add).then_inc(step, 1)
                    dve.wait_ge(step, rows3.after("exponents", g, i))
                    V.tensor_tensor(g_turn, g_turn, g_whole, ALU.subtract).then_inc(step, 1)
                    dve.wait_ge(step, rows3.after("hidden", g, i))
                    V.tensor_scalar(g_z, X1[:, :], vec[:, 4:5], None, ALU.add).then_inc(step, 1)
                    dve.wait_ge(step, rows3.after("ln", g, i))
                    V.scalar_tensor_tensor(g_z, g_z, 0.0, g_y, ALU.max, ALU.add).then_inc(step, 1)
                    dve.wait_ge(step, rows3.after("softplus", g, i))
                    V.tensor_scalar(g_w, g_z, -LOG2, None, ALU.add).then_inc(step, 1)
                    dve.wait_ge(step, rows3.after("cosine", g, i))
                    V.tensor_scalar(g_turn, g_turn, 0.5, 0.5, ALU.mult, ALU.add).then_inc(step, 1)
                    dve.wait_ge(step, rows3.after("raised", g, i))
                    V.tensor_tensor(g_cut, g_turn, g_cut, ALU.mult).then_inc(step, 1)
                    dve.wait_ge(step, rows3.after("cut", g, i))
                    V.scalar_tensor_tensor(g_z, X2[:, :], vec[:, 5:6], g_cut, ALU.add, ALU.mult).then_inc(step, 1)
                    dve.wait_ge(step, rows3.after("weighed", g, i))
                    V.tensor_tensor(four(g_y), four(g_z), bcast(g_yT.rearrange("p (a j) -> p a j", a=1), [F, 4, N]),
                                    ALU.mult).then_inc(step, 1)
                    dve.wait_ge(step, rows3.after("messages", g, i))
                    V.tensor_reduce(g_agg[:, bass.ds(4 * i, 4)], four(g_y), X, ALU.add).then_inc(step, 1)
                dve.wait_ge(rows3.semaphore, rows3.after("kept", g, N // 4 - 1))
                dve.sem_inc(done, 1)
                dve.wait_ge(done, graph.after("hidden3", g))
                V.tensor_scalar(g_norm, X0[:, 0:N], vec[:, 6:7], None, ALU.add).then_inc(done, 1)
                dve.wait_ge(done, graph.after("ln3", g))
                V.scalar_tensor_tensor(g_act, g_norm, 0.0, g_mix, ALU.max, ALU.add).then_inc(done, 1)
                dve.wait_ge(done, graph.after("output3", g))
                V.tensor_tensor(g_sum, X2[:, 0:F], g_x[3], ALU.add).then_inc(done, 1)
                normalize(g, 3)

        def find_verdict(dve):
            V = nc.vector
            dve.wait_ge(s_ck, B)
            dve.wait_ge(s_lc, B)
            dve.wait_ge(s_xaC, B)
            V.tensor_reduce(verdict[:, 0:1], chk_all[:, :], X, ALU.max)
            V.tensor_reduce(verdict[:, 1:2], sum_all[:, :], X, ALU.min)
            V.tensor_reduce(verdict[:, 2:3], deg_all[:, :], X, ALU.min).then_inc(s_verdict, 1)
            dve.wait_ge(s_verdict, 1)
            V.tensor_scalar(verdict[:, 3:4], verdict[:, 0:1], 0.0, None, ALU.is_gt)
            V.tensor_scalar(verdict[:, 4:6], verdict[:, 1:3], 0.0, None, ALU.is_le).then_inc(s_verdict, 1)
            dve.wait_ge(s_vsum, 1)
            V.tensor_reduce(verdict[0:1, 6:7], X0[0:1, 0:3], X, ALU.add).then_inc(s_verdict, 1)
            dve.wait_ge(s_verdict, 3)
            V.tensor_copy(flag[:, :], verdict[0:1, 6:7]).then_inc(s_flag, 1)

        def sum_verdict(pe):
            pe.wait_ge(s_verdict, 2)
            nc.tensor.matmul(X0[0:1, 0:3], ones[:, 0:1], verdict[:, 3:6], start=True, stop=True).then_inc(s_vsum, 1)

        def where_needed(engine, general):
            engine.wait_ge(s_flag, 1)
            count = engine.value_load(flag[0:1, 0:1])
            with engine.If(count > 0):
                general(engine)

        weights = [(ident[:, :], ident_in), (heads[:, :], heads_in), (w0x[:, 0:F], W0), (w1x[:, 0:F], W1),
                   (raw[:, 0, :], W_l), (raw[:, 1, :], W_r), (win[:, :], w_in2f), (w1f[:, :], fw1),
                   (w2f[:, :], fw2), (ow1s[:, :], ow1), (ow2s[:, :], ow2),
                   (vec[:, 0:1], a0.rearrange("(f k) -> f k", k=1)[0:F]),
                   (vec[:, 1:2], a0.rearrange("(f k) -> f k", k=1)[F:2 * F]),
                   (vec[:, 2:3], a1.rearrange("(f k) -> f k", k=1)[0:F]),
                   (vec[:, 3:4], a1.rearrange("(f k) -> f k", k=1)[F:2 * F]),
                   (vec[:, 4:5], fb1.rearrange("(f k) -> f k", k=1)),
                   (vec[:, 5:6], fb2.rearrange("(f k) -> f k", k=1)),
                   (vec[:, 6:7], ob1.rearrange("(f k) -> f k", k=1)),
                   (radial[:, 0:1], widths.rearrange("(f k) -> f k", k=1)),
                   (radial[:, 1:2], offsets.rearrange("(f k) -> f k", k=1)),
                   (brow[:, 1, :], ob2.rearrange("(k f) -> k f", k=1))]
        weights += [(vec[FH * h:FH * (h + 1), 7:8], w_attn.rearrange("(f k) -> f k", k=1)) for h in range(H)]
        LOADS = len(weights)

        def load_first(sp, g):
            wait(sp, s_sm0, g.count(plus=-3), B)
            sp.dma_start(xin[:, g.slot4, :], g.pick(x)).then_inc(s_x[g.slot4], 16)
            wait(sp, s_ck, g.count(plus=-3), B)
            wait(sp, s_xaT, g.count(plus=-3), B)
            sp.dma_start(adj_a[:, g.slot4, :], g.pick(adj)).then_inc(s_aa[g.slot4], 16)

        @block.sync
        def _(sp):
            for to, source in weights:
                sp.dma_start(to, source).then_inc(s_w, 16)

            for k in range(2):
                sp.sem_inc(s_x3k[k], 16)
            for k in range(4):
                sp.sem_inc(s_store[k], 16)
            sp.sem_inc(s_x3T, 1)

            def period(fours, u):
                g = Item(fours, u)
                if g.there():
                    load_first(sp, g)
                g = Item(fours, u - 1)
                if g.there():
                    wait(sp, s_x3T, g.count(plus=-2))
                    sp.dma_start(adj_b[:, g.slot4, :], g.pick(adj)).then_inc(s_ab[g.slot4], 16)
                g = Item(fours, u - 4)
                if g.there():
                    wait(sp, s_x3, g.count(plus=1))
                    sp.dma_start(x3_all[:, g.columns()], x3[:, g.slot2, :]).then_inc(s_x3k[g.slot2], 16)

            for u in range(RING):
                period(0, u)
            with sp.Fori(1, B // RING) as fours:
                for u in range(RING):
                    period(fours, u)
            for u in range(LAST_STAGE):
                period(B // RING, u)
            for k in range(2):
                sp.wait_ge(s_x3k[k], X3_KEPT)
            last_phase_sync(sp)
            where_needed(sp, general_sync)

        @block.tensor
        def _(pe):
            mm = nc.tensor.matmul
            pe.wait_ge(s_w, 16 * LOADS)
            nc.tensor.transpose(X0[:, 0:F], w0x[:, 0:F], ident[:, :])
            nc.tensor.transpose(X0[:, F:2 * F], w1x[:, 0:F], ident[:, :]).then_inc(s_wT, 1)
            pe.wait_ge(s_wTC, 1)
            mm(X1[:, 0:2], raw[:, 2, :], vec[:, 0:2], start=True, stop=True)
            mm(X1[:, 2:4], raw[:, 3, :], vec[:, 2:4], start=True, stop=True).then_inc(s_wa, 1)
            pe.wait_ge(s_scl, 1)
            nc.tensor.transpose(X2[:, 0:F], raw[:, 4, :], ident[:, :])
            nc.tensor.transpose(X2[:, F:2 * F], raw[:, 5, :], ident[:, :])
            nc.tensor.transpose(X2[:, 2 * F:3 * F], raw[:, 1, :], ident[:, :]).then_inc(s_wlr, 1)
            pe.wait_ge(s_rad, 1)
            pe.wait_ge(s_ones, 1)
            mm(T[:, 0:2], w1f[:, :], radial[:, 6:8], start=True, stop=True)
            mm(T[0:1, F:2 * F], ones[:, 0:1], ow2s[:, :], start=True, stop=True).then_inc(s_hid, 1)
            pe.wait_ge(s_row, 1)
            mm(X1[:, 0:F], act1[:, 0, :], ow2s[:, :], start=True, stop=False)
            mm(X1[:, 0:F], ones[0:1, :], brow[0:1, 0, :], start=False, stop=True).then_inc(s_row, 1)
            pe.wait_ge(s_ssp, 1)
            mm(T[:, 2:4], w2f[:, :], filt[:, 6:8], start=True, stop=True).then_inc(s_fil, 1)
            pe.wait_ge(s_ready, 1)

            def pair_sums(g, step):
                half, t = step // 4, step % 4
                wait(pe, s_zv, g.count(STEPS, step + 1))
                wait(pe, s_za, g.count(STEPS, step + 1))
                wait(pe, s_zp, g.count(STEPS, step + 1))
                if t == 0:
                    wait(pe, s_e2, g.count(2, half - 1))
                for c in range(4):
                    last = mm(E[half][32 * c:32 * c + 32, :], ssum[:, t, :],
                              Z[:, half, t, 4 * c:4 * c + 4, :].rearrange("p q j -> p (q j)"),
                              start=(t == 0), stop=False, skip_group_check=True)
                last.then_inc(s_zu, 1)

            def finish_scores(g, half):
                if half == 0:
                    wait(pe, s_mb, g.count(plus=1))
                mm(E[half][:, :].rearrange("p (q j) -> p q j", q=4), slin[:, :, :].rearrange("p m h -> p (m h)"),
                   bcast(gl[:, g.slot2:g.slot2 + 1, :], [F, 4, N]), start=False, stop=False, skip_group_check=True)
                for q in range(4):
                    last = mm(E[half][:, q * N:(q + 1) * N],
                              rows[:, half * 4 + q, :, :].rearrange("p m h -> p (m h)"), maskb[:, g.slot2, :],
                              start=False, stop=(q == 3), skip_group_check=True)
                last.then_inc(s_sc, 1)

            def transpose_probs(g, half):
                wait(pe, s_e2, g.count(2, half + 1))
                wait(pe, s_pC, g.count(2, half))
                for q in range(4):
                    last = nc.tensor.transpose(T[:, q * N:(q + 1) * N], prob2[:, half, q, :], ident[:, :])
                last.then_inc(s_pT, 1)

            def period(fours, u):
                a, b, c, d, e = (Item(fours, u - k) for k in range(5))
                if a.there():
                    pe.wait_ge(s_x[a.slot4], a.loads())
                    pe.wait_ge(s_aa[a.slot4], a.loads())
                    wait(pe, s_grx, a.count(plus=-1))
                    nc.tensor.transpose(X0[:, 0:N], xin[:, a.slot4, :], ident[:, :])
                    nc.tensor.transpose(X0[:, N:2 * N], adj_a[:, a.slot4, :], ident[:, :]).then_inc(s_xaT, 1)
                if e.there():
                    wait(pe, s_x3, e.count(plus=1))
                    pe.wait_ge(s_ab[e.slot4], e.loads())
                    wait(pe, s_mx1, e.count(plus=4), B)
                    nc.tensor.transpose(X2[:, 0:N], x3[:, e.slot2, :], ident[:, :])
                    nc.tensor.transpose(X2[:, N:2 * N], adj_b[:, e.slot4, :], ident[:, :]).then_inc(s_x3T, 1)
                if d.there():
                    pair_sums(d, 7)
                if a.there():
                    wait(pe, s_xaC, a.count(plus=1))
                    mm(X0[:, 0:F + 1], xa[:, a.slot2, 0:N], w0x[:, :], start=True, stop=True)
                    mm(X0[:, 256:384], src0[:, :], xa[:, a.slot2, 0:N], start=True, stop=True).then_inc(s_p0, 1)
                if b.there():
                    wait(pe, s_e1, b.count(plus=1))
                    mm(X1[:, 0:F + 1], prob1[:, b.slot2, :], h1[:, b.slot2, 0:F + 1], start=True, stop=True)
                    mm(X1[:, 256:384], xa[:, b.slot2, N:2 * N], h1[:, b.slot2, 1:F + 1],
                       start=True, stop=True).then_inc(s_at1, 1)
                if e.there():
                    wait(pe, s_x3C, e.count(plus=1))
                    mm(X2[:, 0:F], xa3[:, e.slot2, 0:N], win[:, :], start=True, stop=True).then_inc(s_y3, 1)
                if d.there():
                    finish_scores(d, 1)
                if c.there():
                    pair_sums(c, 0)
                if e.there():
                    wait(pe, s_y3C, e.count(plus=1))
                    mm(X2[:, 128:257], y3[:, e.slot2, :], xa3[:, e.slot2, N:2 * N + 1],
                       start=True, stop=True).then_inc(s_ag3, 1)
                if c.there():
                    pair_sums(c, 1)
                if a.there():
                    wait(pe, s_pr0, a.count(plus=1))
                    mm(X0[:, 0:F + 1], prob0[:, a.slot2, :], h0[:, a.slot2, 0:F + 1],
                       start=True, stop=True).then_inc(s_at0, 1)
                if d.there():
                    transpose_probs(d, 1)
                if c.there():
                    pair_sums(c, 2)
                if d.there():
                    wait(pe, s_pC, d.count(2, 2))
                    wait(pe, s_agC, d.count())
                    for h in range(H):
                        place, k = h % 4, h // 4
                        last = mm(X2[HE * place:HE * (place + 1), k * N:(k + 1) * N], grx[:, d.slot2, h, :],
                                  pT[:, :, :, :, :].rearrange("p c q a (t h) -> p (c q a t) h", h=H)[:, :, h],
                                  start=True, stop=True, skip_group_check=True)
                    last.then_inc(s_sT2, 1)
                if c.there():
                    pair_sums(c, 3)
                if b.there():
                    wait(pe, s_x2, b.count(plus=1))
                    wait(pe, s_sm0, b.count(plus=2), B)
                    nc.tensor.transpose(X0[:, 0:N], x2[:, b.slot4, :], ident[:, :]).then_inc(s_x2T, 1)
                if c.there():
                    finish_scores(c, 0)
                if d.there():
                    wait(pe, s_sT2C, d.count(plus=1))
                    for k in range(2):
                        last = nc.tensor.transpose(X2[:, (2 + k) * N:(3 + k) * N], sT2[:, d.slot2, k * N:(k + 1) * N],
                                                   ident[:, :])
                    last.then_inc(s_at2, 1)
                if a.there():
                    wait(pe, s_x1, a.count(plus=1))
                    wait(pe, s_mix1, a.count())
                    nc.tensor.transpose(X1[:, 0:N], x1[:, a.slot2, :], ident[:, :]).then_inc(s_x1T, 1)
                if c.there():
                    pair_sums(c, 4)
                if a.there():
                    wait(pe, s_x1C, a.count(plus=1))
                    mm(X1[:, 0:F + 1], x1T[:, a.slot2, :], w1x[:, :], start=True, stop=True)
                    mm(X1[:, 256:384], src1[:, :], x1T[:, a.slot2, :], start=True, stop=True)
                    wait(pe, s_nm2, a.count(plus=-2))
                    mm(X2[:, 384:512], dst1[:, :], x1T[:, a.slot2, :], start=True, stop=True).then_inc(s_p1, 1)
                if c.there():
                    pair_sums(c, 5)
                if b.there():
                    wait(pe, s_x2C, b.count(plus=1))
                    wait(pe, s_zv, b.count(STEPS, -STEPS))
                    mm(GL[b.slot2][:, 0:N], wlT[:, :], x2T[:, b.slot2, :], start=True, stop=True)
                    mm(X0[:, 0:N], wrT[:, :], x2T[:, b.slot2, :], start=True, stop=True)
                    mm(X0[:, N:2 * N], x2T[:, b.slot2, :], wrnT[:, :], start=True, stop=True).then_inc(s_p2, 1)
                if c.there():
                    transpose_probs(c, 0)
                    pair_sums(c, 6)

            for u in range(RING):
                period(0, u)
            with pe.Fori(1, B // RING) as fours:
                for u in range(RING):
                    period(fours, u)
            for u in range(LAST_STAGE + 1):
                period(B // RING, u)
            last_phase_tensor(pe)
            sum_verdict(pe)
            where_needed(pe, general_tensor)

        @block.scalar
        def _(act):
            A = nc.scalar.activation
            nc.scalar.preload_act_table_set("natural_log_exp_and_others")
            act.wait_ge(s_w, 16 * LOADS)
            act.wait_ge(s_rade, 1)
            A(radial[:, 6:8], radial[:, 4:6], ACT.Exp).then_inc(s_rad, 1)
            act.wait_ge(s_hidb, 1)
            A(filt[:, 2:4], filt[:, 0:2], ACT.Abs).then_inc(s_soft, 1)
            act.wait_ge(s_soft, 1)
            A(filt[:, 2:4], filt[:, 2:4], ACT.Exp, scale=-1.0).then_inc(s_soft, 1)
            act.wait_ge(s_soft, 2)
            A(filt[:, 4:6], filt[:, 2:4], ACT.Ln, bias=1.0).then_inc(s_soft, 1)
            act.wait_ge(s_ready, 1)
            nc.scalar.preload_act_table_set("exp_and_others")

            def tiles(g, step):
                half, t = step // 4, step % 4
                wait(act, s_zu, g.count(STEPS, step + 1 - STEPS))
                for k in range(DVE_TILES[step], DVE_TILES[step] + ACT_TILES[step]):
                    i = 8 * k + step
                    A(Z[:, half, t, k, :], gl[:, g.slot2, :], ACT.Relu, bias=gr[:, g.slot2, i:i + 1])

            def finish_tiles(g, step):
                half, t = step // 4, step % 4
                first = DVE_TILES[step] + ACT_TILES[step]
                wait(act, s_zp, g.count(STEPS, step + 1))
                A(Z[:, half, t, first:TILES, :], Z[:, half, t, first:TILES, :], ACT.Relu).then_inc(s_za, 1)

            def exps(g, half):
                wait(act, s_mx2, g.count(2, half + 1))
                wait(act, s_pT, g.count(2, half - 1))
                for q in range(4):
                    ins = A(prob2[:, half, q, :], E[half][:, q * N:(q + 1) * N], ACT.Exp,
                            bias=negmax[:, g.slot2, half * 4 + q:half * 4 + q + 1])
                ins.then_inc(s_e2, 1)

            def copy_probs(g, half):
                wait(act, s_pT, g.count(2, half + 1))
                wait(act, s_at2, g.count())
                A(pT[:, :, :, half, :].rearrange("p c q k -> p q c k"),
                  T[:, :].rearrange("p (q c k) -> p q c k", q=4, c=4), ACT.Copy).then_inc(s_pC, 1)

            def period(fours, u):
                a, b, c, d, e = (Item(fours, u - k) for k in range(5))
                on = c.there()
                if d.there():
                    finish_tiles(d, 7)
                if on:
                    wait(act, s_gl, c.count(plus=1))
                    wait(act, s_gr, c.count(plus=1))
                    tiles(c, 0)
                if a.there():
                    wait(act, s_xaT, a.count(plus=1))
                    wait(act, s_p0, a.count(plus=-1))
                    wait(act, s_at1, a.count(plus=-1))
                    A(xa[:, a.slot2, 0:N], X0[:, 0:N], ACT.Copy)
                    A(xa[:, a.slot2, N:2 * N], X0[:, N:2 * N], ACT.Copy,
                      accum_out=deg_all[:, a.columns(1)]).then_inc(s_xaC, 1)
                if b.there():
                    wait(act, s_d1, b.count(plus=1))
                    wait(act, s_dt1, b.count(plus=1))
                    A(prob1[:, b.slot2, :], dif1[:, b.slot2, :], ACT.Exp, scale=1.0 - SLOPE,
                      bias=small[:, b.slot2, 23:24]).then_inc(s_e1, 1)
                if e.there():
                    wait(act, s_x3T, e.count(plus=2))
                    A(xa3[:, e.slot2, 0:2 * N], X2[:, 0:2 * N], ACT.Copy).then_inc(s_x3C, 1)
                if on:
                    finish_tiles(c, 0)
                if b.there():
                    wait(act, s_at1, b.count(plus=1))
                    A(nbr1[:, b.slot2, :], X1[:, 256:384], ACT.Copy).then_inc(s_nb1, 1)
                if on:
                    tiles(c, 1)
                if a.there():
                    wait(act, s_p0, a.count(plus=1))
                    A(h0[:, a.slot2, 1:F + 2], X0[:, 0:F + 1], ACT.Copy).then_inc(s_h0, 1)
                if a.there():
                    wait(act, s_h0, a.count(plus=1))
                    A(tanh0[:, a.slot2, :], X0[:, 256:384], ACT.Tanh,
                      bias=h0[:, a.slot2, F + 1:F + 2]).then_inc(s_th, 1)
                if e.there():
                    wait(act, s_y3, e.count(plus=1))
                    A(y3[:, e.slot2, :], X2[:, 0:F], ACT.Copy).then_inc(s_y3C, 1)
                if a.there():
                    wait(act, s_th, a.count(plus=1))
                    A(exp0[:, a.slot2, :], tanh0[:, a.slot2, :], ACT.Exp).then_inc(s_e0, 1)
                if on:
                    finish_tiles(c, 1)
                    tiles(c, 2)
                if e.there():
                    wait(act, s_ag3, e.count(plus=1))
                    A(ysum[:, e.slot2, :], X2[:, 256:257], ACT.Copy, scale=filt[:, 8:9]).then_inc(s_ys, 1)
                if d.there():
                    exps(d, 1)
                if on:
                    finish_tiles(c, 2)
                    tiles(c, 3)
                if e.there():
                    wait(act, s_ys, e.count(plus=1))
                    A(agg_all[:, e.columns()], X2[:, 128:256], ACT.Identity, scale=filt[:, 9:10],
                      bias=ysum[:, e.slot2, :]).then_inc(s_agC, 1)
                if d.there():
                    copy_probs(d, 1)
                if on:
                    finish_tiles(c, 3)
                    tiles(c, 4)
                if d.there():
                    wait(act, s_sT2, d.count(plus=1))
                    A(sT2[:, d.slot2, :], X2[:, 0:2 * N], ACT.Copy).then_inc(s_sT2C, 1)
                if on:
                    finish_tiles(c, 4)
                    tiles(c, 5)
                if b.there():
                    wait(act, s_x2T, b.count(plus=1))
                    A(x2T[:, b.slot2, :], X0[:, 0:N], ACT.Copy).then_inc(s_x2C, 1)
                if on:
                    finish_tiles(c, 5)
                    tiles(c, 6)
                if a.there():
                    wait(act, s_x1T, a.count(plus=1))
                    A(x1T[:, a.slot2, :], X1[:, 0:N], ACT.Copy).then_inc(s_x1C, 1)
                if on:
                    finish_tiles(c, 6)
                    tiles(c, 7)
                if a.there():
                    wait(act, s_p1, a.count(plus=1))
                    A(h1[:, a.slot2, 1:F + 2], X1[:, 0:F + 1], ACT.Copy).then_inc(s_h1, 1)
                if c.there():
                    exps(c, 0)
                if a.there():
                    wait(act, s_h1, a.count(plus=1))
                    A(relu1[:, a.slot2, :], X1[:, 256:384], ACT.Relu,
                      bias=h1[:, a.slot2, F + 1:F + 2]).then_inc(s_u1, 1)
                if b.there():
                    wait(act, s_p2, b.count(plus=1))
                    wait(act, s_sc, b.count(2, -2))
                    wait(act, s_zp, b.count(STEPS, -STEPS))
                    wait(act, s_zv, b.count(STEPS, -STEPS))
                    wait(act, s_at2, b.count(plus=-1))
                    A(gl[:, b.slot2, :], GL[b.slot2][:, 0:N], ACT.Copy).then_inc(s_gl, 1)
                    A(gr[:, b.slot2, :], X0[:, 0:N], ACT.Copy).then_inc(s_gr, 1)
                    A(ngr[:, b.slot2, :], X0[:, 0:N], ACT.Copy, scale=-1.0).then_inc(s_ngr, 1)
                    A(grx[:, b.slot2, :, 0:FH], X0[:, N:2 * N].rearrange("p (h f) -> p h f", h=H),
                      ACT.Copy).then_inc(s_grx, 1)
                if a.there():
                    wait(act, s_mx1, a.count(plus=1))
                    A(max1[:, a.slot2, :], X1[:, 256:384], ACT.Relu,
                      bias=small[:, a.slot2, 20:21]).then_inc(s_m1, 1)
                if c.there():
                    copy_probs(c, 0)

            for u in range(RING):
                period(0, u)
            with act.Fori(1, B // RING) as fours:
                for u in range(RING):
                    period(fours, u)
            for u in range(LAST_STAGE + 1):
                period(B // RING, u)
            last_phase_scalar(act)
            where_needed(act, general_scalar)

        @block.vector
        def _(dve):
            V = nc.vector
            V.memset(ones[:, :], 1.0).then_inc(s_ones, 1)
            for k in range(2):
                V.memset(h0[:, k, 0:1], 1.0)
                V.memset(h1[:, k, 0:1], 1.0)
                V.memset(grx[:, k, :, FH:HE], 1.0)
                V.memset(xa3[:, k, 2 * N:2 * N + 1], 1.0)
            V.memset(ssum[:, :, :], 0.0).then_inc(s_ones, 1)
            dve.wait_ge(s_w, 16 * LOADS)
            dve.wait_ge(s_wT, 1)
            V.tensor_copy(raw[:, 2:4, :].rearrange("p k f -> p (k f)"), X0[:, 0:2 * F]).then_inc(s_wTC, 1)
            V.tensor_scalar(sgn[:, 0:1], vec[:, 7:8], 0.0, None, ALU.is_gt)
            V.tensor_scalar(sgn[:, 1:2], vec[:, 7:8], 0.0, None, ALU.is_lt).then_inc(s_own, 1)
            dve.wait_ge(s_own, 1)
            V.tensor_tensor(sgn[:, 2:3], sgn[:, 0:1], sgn[:, 1:2], ALU.subtract).then_inc(s_own, 1)
            dve.wait_ge(s_own, 2)
            V.scalar_tensor_tensor(sgn[:, 3:4], sgn[:, 2:3], 1.0 - SLOPE, vec[:, 7:8], ALU.mult, ALU.mult)\
                .then_inc(s_own, 1)
            dve.wait_ge(s_own, 3)
            V.tensor_scalar(raw[:, 4, :], raw[:, 0, :], sgn[:, 3:4], None, ALU.mult)
            V.tensor_scalar(raw[:, 5, :], raw[:, 1, :], sgn[:, 3:4], None, ALU.mult).then_inc(s_scl, 1)
            V.tensor_scalar(sgn8[:, :], heads[:, :], sgn[:, 2:3], None, ALU.mult).then_inc(s_own, 1)
            dve.wait_ge(s_own, 4)
            dve.wait_ge(s_ones, 2)
            for t in range(4):
                V.tensor_copy(ssum[:, t, t * H:(t + 1) * H], sgn8[:, :])
            for m in range(16):
                V.tensor_scalar(slin[:, m, :], sgn8[:, :], SLOPE / (1.0 - SLOPE), None, ALU.mult)
            for half in range(2):
                for q in range(4):
                    picked = ident[:, :].rearrange("p (c q a t k) -> p c q a t k", c=4, q=4, a=2, k=1)[:, :, q, half]
                    V.tensor_copy(rows[:, half * 4 + q, :, :].rearrange("p (c t) h -> p c t h", c=4),
                                  bcast(picked, [N, 4, 4, H]))
            dve.wait_ge(s_wa, 1)
            V.tensor_copy(wcol[:, :], X1[:, 0:4]).then_inc(s_own, 1)
            dve.wait_ge(s_own, 5)
            V.tensor_copy(w0x[:, F:F + 1], wcol[:, 1:2])
            V.tensor_copy(w1x[:, F:F + 1], wcol[:, 3:4])
            V.tensor_copy(src0[:, :], bcast(wcol[:, 0:1], [F, N]))
            V.tensor_copy(src1[:, :], bcast(wcol[:, 2:3], [F, N]))
            V.tensor_copy(dst1[:, :], bcast(wcol[:, 3:4], [F, N]))
            dve.wait_ge(s_wlr, 1)
            V.tensor_copy(wlT[:, :], X2[:, 0:F])
            V.tensor_copy(wrT[:, :], X2[:, F:2 * F])
            V.tensor_copy(wrnT[:, :], X2[:, 2 * F:3 * F])
            V.tensor_tensor(radial[:, 2:3], radial[:, 0:1], radial[:, 0:1], ALU.mult)
            V.tensor_scalar(radial[:, 4:5], radial[:, 1:2], -1.0, None, ALU.mult).then_inc(s_own, 1)
            dve.wait_ge(s_own, 6)
            V.reciprocal(radial[:, 3:4], radial[:, 2:3])
            V.tensor_scalar(radial[:, 5:6], radial[:, 4:5], 1.0, None, ALU.add).then_inc(s_own, 1)
            dve.wait_ge(s_own, 7)
            V.tensor_tensor(radial[:, 4:6], radial[:, 4:6], radial[:, 4:6], ALU.mult).then_inc(s_own, 1)
            dve.wait_ge(s_own, 8)
            V.tensor_scalar(radial[:, 4:6], radial[:, 4:6], radial[:, 3:4], -0.5, ALU.mult, ALU.mult)\
                .then_inc(s_rade, 1)
            dve.wait_ge(s_hid, 1)
            V.tensor_scalar(filt[:, 0:2], T[:, 0:2], vec[:, 4:5], None, ALU.add).then_inc(s_hidb, 1)
            V.scalar_tensor_tensor(brow[0:1, 0, :], T[0:1, F:2 * F], -LOG2, brow[0:1, 1, :], ALU.mult, ALU.add)
            V.tensor_scalar(vec[:, 8:9], vec[:, 6:7], -1.0, None, ALU.mult)
            V.tensor_copy(act1[:, 0, :], bcast(vec[:, 6:7], [F, N])).then_inc(s_row, 1)
            dve.wait_ge(s_row, 2)
            V.tensor_copy(rowb[:, :], X1[:, 0:F])
            dve.wait_ge(s_soft, 3)
            V.scalar_tensor_tensor(filt[:, 6:8], filt[:, 0:2], 0.0, filt[:, 4:6], ALU.max, ALU.add).then_inc(s_own, 1)
            dve.wait_ge(s_own, 9)
            V.tensor_scalar(filt[:, 6:8], filt[:, 6:8], -LOG2, None, ALU.add).then_inc(s_ssp, 1)
            dve.wait_ge(s_fil, 1)
            V.tensor_scalar(filt[:, 8:9], T[:, 2:3], vec[:, 5:6], CUT0, ALU.add, ALU.mult)
            V.tensor_scalar(filt[:, 10:11], T[:, 3:4], vec[:, 5:6], CUT1, ALU.add, ALU.mult).then_inc(s_own, 1)
            dve.wait_ge(s_own, 10)
            V.tensor_tensor(filt[:, 9:10], filt[:, 10:11], filt[:, 8:9], ALU.subtract).then_inc(s_ready, 1)
            dve.wait_ge(s_ready, 1)

            def tiles(g, step):
                half, t = step // 4, step % 4
                count = DVE_TILES[step]
                wait(dve, s_zu, g.count(STEPS, step + 1 - STEPS))
                minus_gr = ngr[:, g.slot2, :].rearrange("p (i s) -> p i s", s=8)[:, 0:count, step:step + 1]
                V.tensor_tensor(Z[:, half, t, 0:count, :],
                                bcast(GL[g.slot2][:, 0:N].rearrange("p (a j) -> p a j", a=1), [F, count, N]),
                                bcast(minus_gr, [F, count, N]), ALU.max).then_inc(s_zv, 1)

            def moments(g, data, at, s_data, s_stats):
                wait(dve, s_data, g.count(plus=1))
                V.bn_stats(small[:, g.slot2, at:at + 6], data).then_inc(s_stats, 1)

            def variance(g, at, s_var):
                V.bn_aggr(small[:, g.slot2, at + 6:at + 8], small[:, g.slot2, at:at + 6]).then_inc(s_var, 1)

            def period(fours, u):
                a, b, c, d, e = (Item(fours, u - k) for k in range(5))
                on = c.there()
                if on:
                    wait(dve, s_gl, c.count(plus=1))
                    wait(dve, s_ngr, c.count(plus=1))
                    tiles(c, 0)
                if a.there():
                    dve.wait_ge(s_aa[a.slot4], a.loads())
                    V.scalar_tensor_tensor(chk[:, a.slot2, :], adj_a[:, a.slot4, :], 1.0, adj_a[:, a.slot4, :],
                                           ALU.is_equal, ALU.not_equal, accum_out=chk_all[:, a.columns(1)])\
                        .then_inc(s_ck, 1)
                if on:
                    tiles(c, 1)
                if b.there():
                    wait(dve, s_nb1, b.count(plus=1))
                    V.reciprocal(small[:, b.slot2, 21:22], X1[:, 0:1]).then_inc(s_rs1, 1)
                    wait(dve, s_rs1, b.count(plus=1))
                    V.scalar_tensor_tensor(mix1[:, b.slot2, :], X1[:, 1:F + 1], small[:, b.slot2, 21:22],
                                           nbr1[:, b.slot2, :], ALU.mult, ALU.add).then_inc(s_mix1, 1)
                    wait(dve, s_mix1, b.count(plus=1))
                    V.scalar_tensor_tensor(act1[:, b.slot2, :], mix1[:, b.slot2, :], SLOPE, mix1[:, b.slot2, :],
                                           ALU.mult, ALU.max).then_inc(s_act1, 1)
                    wait(dve, s_act1, b.count(plus=1))
                    V.tensor_tensor(sum1[:, b.slot2, :], act1[:, b.slot2, :], x1[:, b.slot2, :], ALU.add)\
                        .then_inc(s_sm1, 1)
                    moments(b, sum1[:, b.slot2, :], 32, s_sm1, s_st1)
                    wait(dve, s_st1, b.count(plus=1))
                if d.there():
                    wait(dve, s_sc, d.count(2, 2))
                    V.tensor_reduce(negmax[:, d.slot2, 4:8], E[1][:, :].rearrange("p (q j) -> p q j", q=4), X, ALU.max,
                                    negate=True).then_inc(s_mx2, 1)
                if on:
                    tiles(c, 2)
                if b.there():
                    variance(b, 32, s_ag1)
                if on:
                    tiles(c, 3)
                if a.there():
                    wait(dve, s_at0, a.count(plus=1))
                    V.reciprocal(small[:, a.slot2, 22:23], X0[:, 0:1]).then_inc(s_rs0, 1)
                    V.tensor_copy(sum_all[:, a.columns(1)], X0[:, 0:1]).then_inc(s_lc, 1)
                if a.there():
                    wait(dve, s_rs0, a.count(plus=1))
                    V.scalar_tensor_tensor(sum0[:, a.slot2, :], X0[:, 1:F + 1], small[:, a.slot2, 22:23],
                                           xin[:, a.slot4, :], ALU.mult, ALU.add).then_inc(s_sm0, 1)
                    moments(a, sum0[:, a.slot2, :], 0, s_sm0, s_st0)
                    wait(dve, s_st0, a.count(plus=1))
                if b.there():
                    wait(dve, s_rd1, b.count(plus=1))
                    V.tensor_scalar(x2[:, b.slot4, :], sum1[:, b.slot2, :], small[:, b.slot2, 38:39],
                                    small[:, b.slot2, 41:42], ALU.subtract, ALU.mult).then_inc(s_x2, 1)
                if a.there():
                    variance(a, 0, s_ag0)
                if on:
                    tiles(c, 4)
                if a.there():
                    wait(dve, s_rd0, a.count(plus=1))
                    V.tensor_scalar(x1[:, a.slot2, :], sum0[:, a.slot2, :], small[:, a.slot2, 6:7],
                                    small[:, a.slot2, 9:10], ALU.subtract, ALU.mult).then_inc(s_x1, 1)
                if on:
                    tiles(c, 5)
                if d.there():
                    wait(dve, s_at2, d.count(plus=1))
                    V.reciprocal(small[:, d.slot2, 24:32],
                                 X2[:, 2 * N:4 * N].rearrange("p (h f) -> p h f", h=H)[:, :, FH]).then_inc(s_rs2, 1)
                    wait(dve, s_rs2, d.count(plus=1))
                    V.tensor_tensor(att2[:, d.slot2, :, :],
                                    X2[:, 2 * N:4 * N].rearrange("p (h f) -> p h f", h=H)[:, :, 0:FH],
                                    bcast(small[:, d.slot2, 24:32].rearrange("p (h k) -> p h k", k=1), [N, H, FH]),
                                    ALU.mult).then_inc(s_nm2, 1)
                    wait(dve, s_nm2, d.count(plus=1))
                    flat = att2[:, d.slot2, :, :].rearrange("p h f -> p (h f)")
                    V.scalar_tensor_tensor(act2[:, d.slot2, :], flat, SLOPE, flat, ALU.mult, ALU.max)\
                        .then_inc(s_act2, 1)
                    wait(dve, s_act2, d.count(plus=1))
                    V.tensor_tensor(sum2[:, d.slot2, :], act2[:, d.slot2, :], x2[:, d.slot4, :], ALU.add)\
                        .then_inc(s_sm2, 1)
                    moments(d, sum2[:, d.slot2, :], 48, s_sm2, s_st2)
                    wait(dve, s_st2, d.count(plus=1))
                if on:
                    wait(dve, s_sc, c.count(2, 1))
                    V.tensor_reduce(negmax[:, c.slot2, 0:4], E[0][:, :].rearrange("p (q j) -> p q j", q=4), X, ALU.max,
                                    negate=True).then_inc(s_mx2, 1)
                if d.there():
                    variance(d, 48, s_ag2)
                if on:
                    tiles(c, 6)
                if a.there():
                    wait(dve, s_p1, a.count(plus=1))
                    V.tensor_reduce(small[:, a.slot2, 20:21], X2[:, 384:512], X, ALU.max).then_inc(s_mx1, 1)
                if on:
                    tiles(c, 7)
                if d.there():
                    wait(dve, s_rd2, d.count(plus=1))
                    wait(dve, s_x3k[d.slot2], d.loads(2))
                    V.tensor_scalar(x3[:, d.slot2, :], sum2[:, d.slot2, :], small[:, d.slot2, 54:55],
                                    small[:, d.slot2, 57:58], ALU.subtract, ALU.mult).then_inc(s_x3, 1)
                if a.there():
                    wait(dve, s_h1, a.count(plus=1))
                    wait(dve, s_mx1, a.count(plus=1))
                    V.tensor_scalar(small[:, a.slot2, 23:24], h1[:, a.slot2, F + 1:F + 2], small[:, a.slot2, 20:21],
                                    SLOPE, ALU.subtract, ALU.mult).then_inc(s_dt1, 1)

            for u in range(RING):
                period(0, u)
            with dve.Fori(1, B // RING) as fours:
                for u in range(RING):
                    period(fours, u)
            for u in range(LAST_STAGE):
                period(B // RING, u)
            last_phase_vector(dve)
            find_verdict(dve)
            where_needed(dve, general_vector)

        @block.gpsimd
        def _(pool):
            G = nc.gpsimd
            G.memset(epses[:, :], EPS)
            G.memset(halves[:, :], -0.5).then_inc(s_cst, 1)
            pool.wait_ge(s_cst, 1)

            def tiles(g, step):
                half, t = step // 4, step % 4
                first = DVE_TILES[step] + ACT_TILES[step]
                wait(pool, s_zu, g.count(STEPS, step + 1 - STEPS))
                minus_gr = ngr[:, g.slot2, :].rearrange("p (i s) -> p i s", s=8)[:, first:TILES, step:step + 1]
                G.tensor_tensor(Z[:, half, t, first:TILES, :], bcast(gl[:, g.slot2:g.slot2 + 1, :], [F, TILES - first, N]),
                                bcast(minus_gr, [F, TILES - first, N]), ALU.subtract).then_inc(s_zp, 1)

            def rstd(g, at, s_var, s_eps, s_rstd):
                wait(pool, s_var, g.count(plus=1))
                G.tensor_tensor(small[:, g.slot2, at + 8:at + 9], small[:, g.slot2, at + 7:at + 8], epses[:, 0:1],
                                ALU.add).then_inc(s_eps, 1)
                wait(pool, s_eps, g.count(plus=1))
                G.tensor_tensor(small[:, g.slot2, at + 9:at + 10], small[:, g.slot2, at + 8:at + 9], halves[:, 0:1],
                                ALU.pow).then_inc(s_rstd, 1)

            def period(fours, u):
                a, b, c, d, e = (Item(fours, u - k) for k in range(5))
                on = c.there()
                if on:
                    wait(pool, s_gl, c.count(plus=1))
                    wait(pool, s_ngr, c.count(plus=1))
                    for step in range(4):
                        tiles(c, step)
                if c.there():
                    pool.wait_ge(s_ab[c.slot4], c.loads())
                    wait(pool, s_sc, c.count(2, -2))
                if a.there():
                    wait(pool, s_e0, a.count(plus=1))
                    wait(pool, s_at0, a.count(plus=-1))
                    G.tensor_tensor(prob0[:, a.slot2, :], exp0[:, a.slot2, :], xa[:, a.slot2, N:2 * N], ALU.mult)\
                        .then_inc(s_pr0, 1)
                if c.there():
                    G.tensor_scalar(maskb[:, c.slot2, :], adj_b[:, c.slot4, :], MASKED, -MASKED, ALU.mult, ALU.add)\
                        .then_inc(s_mb, 1)
                if b.there():
                    rstd(b, 32, s_ag1, s_ve1, s_rd1)
                if on:
                    tiles(c, 4)
                if a.there():
                    rstd(a, 0, s_ag0, s_ve0, s_rd0)
                if on:
                    tiles(c, 5)
                    tiles(c, 6)
                if d.there():
                    rstd(d, 48, s_ag2, s_ve2, s_rd2)
                if on:
                    tiles(c, 7)
                if a.there():
                    wait(pool, s_u1, a.count(plus=1))
                    wait(pool, s_m1, a.count(plus=1))
                    G.tensor_tensor(dif1[:, a.slot2, :], relu1[:, a.slot2, :], max1[:, a.slot2, :], ALU.subtract)\
                        .then_inc(s_d1, 1)

            for u in range(RING):
                period(0, u)
            with pool.Fori(1, B // RING) as fours:
                for u in range(RING):
                    period(fours, u)
            for u in range(LAST_STAGE):
                period(B // RING, u)
            last_phase_pool(pool)
            where_needed(pool, general_pool)


_INS = ["x", "adj", "L0_gnn_W", "L0_gnn_a", "L1_gnn_W", "L1_gnn_a", "L2_gnn_W_l", "L2_gnn_W_r", "L2_gnn_w_attn",
        "L3_gnn_widths", "L3_gnn_offsets", "L3_gnn_w_in2f", "L3_gnn_fw1", "L3_gnn_fb1", "L3_gnn_fw2", "L3_gnn_fb2",
        "L3_gnn_ow1", "L3_gnn_ob1", "L3_gnn_ow2", "L3_gnn_ob2"]


def kernel(**inputs):
    import numpy as _np
    import concourse.bacc as _bacc
    from concourse import mybir as _mybir
    from concourse.bass_utils import run_bass_kernel_spmd as _run

    nc = _bacc.Bacc("TRN2", target_bir_lowering=False, num_devices=1)
    arrays, args = {}, []
    for name in _INS:
        arrays[name + "_dram"] = _np.ascontiguousarray(inputs[name])
    arrays["ident_dram"] = _np.eye(N, dtype=_np.float32)
    arrays["heads_dram"] = _np.repeat(_np.eye(H, dtype=_np.float32), FH, axis=0)
    for name, a in arrays.items():
        args.append(nc.dram_tensor(name, a.shape, _mybir.dt.from_np(a.dtype), kind="ExternalInput").ap())
    out = nc.dram_tensor("out_dram", (B, N, F), FP32, kind="ExternalOutput").ap()
    build(nc, *args, out)
    r = _run(nc, [arrays], core_ids=[0])
    return r.results[0]["out_dram"]
```
